# Optimizing a Trainium2 kernel written in Bass

```python
import numpy as np
import jax
import jax.numpy as jnp

def _softmax(x, axis=-1):
    return jax.nn.softmax(x, axis=axis)
def _gelu(x):
    return jax.nn.gelu(x, approximate=True)
def _silu(x):
    return jax.nn.silu(x)
def _sigmoid(x):
    return jax.nn.sigmoid(x)
def _layernorm(x, axis=-1, eps=1e-5):
    m = jnp.mean(x, axis=axis, keepdims=True)
    v = jnp.var(x, axis=axis, keepdims=True)
    return (x - m) / jnp.sqrt(v + eps)
def _scatter_add(tgt, idx, src, axis=0):
    return tgt.at[idx].add(src)
def _segment_sum(src, seg, n):
    return jax.ops.segment_sum(src, seg, n)

kernel_name = 'mk_conv_seq_d2_conv_nhwc192_eb567d'

def setup_inputs(seed: int = 0):
    np.random.seed(seed)
    _w = jnp.asarray
    def _rec_inputs():
        import jax
        import jax.numpy as jnp
        _gk = jax.random.key(seed)
        x = -0.0001538 + 1 * jax.random.normal(jax.random.fold_in(_gk, 1), (8, 64, 64, 192), jnp.float32)
        return x
    x = _rec_inputs()
    def _L0_conv_setup():
        import jax, jax.numpy as jnp
        import numpy as np
        C = 192
        RATIO = 8
        DQK = C // RATIO
        DV = C // RATIO
        B, H, W = (8, 64, 64)
        key = jax.random.key(seed)
        ks = jax.random.split(key, 5)
        tensor = jax.random.normal(ks[0], (B, H, W, C), dtype=jnp.float32)
        w_q = jax.random.normal(ks[1], (C, DQK), dtype=jnp.float32) * (1.0 / np.sqrt(C))
        w_k = jax.random.normal(ks[2], (C, DQK), dtype=jnp.float32) * (1.0 / np.sqrt(C))
        w_v = jax.random.normal(ks[3], (C, DV), dtype=jnp.float32) * (1.0 / np.sqrt(C))
        w_o = jax.random.normal(ks[4], (DV, C), dtype=jnp.float32) * (1.0 / np.sqrt(DV))
        gamma = jnp.float32(0.1)
        return {'tensor': tensor, 'w_q': w_q, 'w_k': w_k, 'w_v': w_v, 'w_o': w_o, 'gamma': gamma}
    _L0_conv_all = _L0_conv_setup()
    _L0_conv_in = {k: v for k, v in _L0_conv_all.items() if k in ('w_q', 'w_k', 'w_v', 'w_o', 'gamma', )}
    del _L0_conv_all

    def _L1_conv_setup():
        import jax, jax.numpy as jnp
        import numpy as np
        from jax import lax
        B, H, W, C = (32, 64, 64, 192)
        DIN = 2 * C
        EPS = 1e-05

        def _scan_dir(x, d):
            b, h, w, c = x.shape
            if d == 0:
                return x.reshape(b, h * w, c)
            if d in (1, 2):
                return x.transpose(0, 2, 1, 3).reshape(b, w * h, c)
            return jnp.flip(x, axis=2).transpose(0, 2, 1, 3).reshape(b, w * h, c)

        def _seq_block(s, fc1_w, fc1_b, conv_w, conv_b, fc2_w, fc2_b):
            h = jnp.einsum('blc,dc->bld', s, fc1_w) + fc1_b
            hc = h.transpose(0, 2, 1)
            hc = lax.conv_general_dilated(hc, conv_w, window_strides=(1,), padding=[(1, 1)], dimension_numbers=('NCH', 'OIH', 'NCH'), feature_group_count=conv_w.shape[0])
            hc = hc + conv_b[None, :, None]
            h = jax.nn.gelu(hc.transpose(0, 2, 1), approximate=False)
            return jnp.einsum('bld,cd->blc', h, fc2_w) + fc2_b
        key = jax.random.key(seed)
        ks = jax.random.split(key, 12)
        s = 0.02
        return {'x': jax.random.normal(ks[0], (B, H, W, C), dtype=jnp.float32), 'norm_w': jnp.ones((C,), jnp.float32), 'norm_b': jnp.zeros((C,), jnp.float32), 'sel_w1': jax.random.normal(ks[1], (16, 4), jnp.float32) * 0.5, 'sel_b1': jnp.zeros((16,), jnp.float32), 'sel_w2': jax.random.normal(ks[2], (4, 16), jnp.float32) * 0.5, 'sel_b2': jnp.zeros((4,), jnp.float32), 'fc1_w': jax.random.normal(ks[3], (DIN, C), jnp.float32) * s, 'fc1_b': jnp.zeros((DIN,), jnp.float32), 'conv_w': jax.random.normal(ks[4], (DIN, 1, 3), jnp.float32) * 0.3, 'conv_b': jnp.zeros((DIN,), jnp.float32), 'fc2_w': jax.random.normal(ks[5], (C, DIN), jnp.float32) * s, 'fc2_b': jnp.zeros((C,), jnp.float32)}
    _L1_conv_all = _L1_conv_setup()
    _L1_conv_in = {k: v for k, v in _L1_conv_all.items() if k in ('norm_w', 'norm_b', 'sel_w1', 'sel_b1', 'sel_w2', 'sel_b2', 'fc1_w', 'fc1_b', 'conv_w', 'conv_b', 'fc2_w', 'fc2_b', )}
    del _L1_conv_all

    return {
        "x": x,
        "L0_conv_w_q": _L0_conv_in["w_q"],
        "L0_conv_w_k": _L0_conv_in["w_k"],
        "L0_conv_w_v": _L0_conv_in["w_v"],
        "L0_conv_w_o": _L0_conv_in["w_o"],
        "L0_conv_gamma": _L0_conv_in["gamma"],
        "L1_conv_norm_w": _L1_conv_in["norm_w"],
        "L1_conv_norm_b": _L1_conv_in["norm_b"],
        "L1_conv_sel_w1": _L1_conv_in["sel_w1"],
        "L1_conv_sel_b1": _L1_conv_in["sel_b1"],
        "L1_conv_sel_w2": _L1_conv_in["sel_w2"],
        "L1_conv_sel_b2": _L1_conv_in["sel_b2"],
        "L1_conv_fc1_w": _L1_conv_in["fc1_w"],
        "L1_conv_fc1_b": _L1_conv_in["fc1_b"],
        "L1_conv_conv_w": _L1_conv_in["conv_w"],
        "L1_conv_conv_b": _L1_conv_in["conv_b"],
        "L1_conv_fc2_w": _L1_conv_in["fc2_w"],
        "L1_conv_fc2_b": _L1_conv_in["fc2_b"],
    }

def reference(x, L0_conv_w_q, L0_conv_w_k, L0_conv_w_v, L0_conv_w_o, L0_conv_gamma, L1_conv_norm_w, L1_conv_norm_b, L1_conv_sel_w1, L1_conv_sel_b1, L1_conv_sel_w2, L1_conv_sel_b2, L1_conv_fc1_w, L1_conv_fc1_b, L1_conv_conv_w, L1_conv_conv_b, L1_conv_fc2_w, L1_conv_fc2_b):
    import jax
    import jax.numpy as jnp
    def _L0_conv_ref(tensor, w_q, w_k, w_v, w_o, gamma):
        import jax, jax.numpy as jnp
        import numpy as np
        C = 192
        RATIO = 8
        DQK = C // RATIO
        DV = C // RATIO
        B, H, W = (8, 64, 64)
        b, h, w, c = tensor.shape
        L = h * w
        q = jnp.einsum('bhwc,cd->bhwd', tensor, w_q).reshape(b, L, DQK)
        k = jnp.einsum('bhwc,cd->bhwd', tensor, w_k).reshape(b, L, DQK)
        v = jnp.einsum('bhwc,cd->bhwd', tensor, w_v).reshape(b, L, DV)
        scores = jnp.einsum('bqd,bkd->bqk', q, k)
        beta = jax.nn.softmax(scores, axis=-1)
        attn = jnp.einsum('bqk,bkd->bqd', beta, v).reshape(b, h, w, DV)
        out = gamma * jnp.einsum('bhwd,dc->bhwc', attn, w_o)
        return out + tensor

    def _L1_conv_ref(x, norm_w, norm_b, sel_w1, sel_b1, sel_w2, sel_b2, fc1_w, fc1_b, conv_w, conv_b, fc2_w, fc2_b):
        import jax, jax.numpy as jnp
        import numpy as np
        from jax import lax
        B, H, W, C = (32, 64, 64, 192)
        DIN = 2 * C
        EPS = 1e-05

        def _scan_dir(x, d):
            b, h, w, c = x.shape
            if d == 0:
                return x.reshape(b, h * w, c)
            if d in (1, 2):
                return x.transpose(0, 2, 1, 3).reshape(b, w * h, c)
            return jnp.flip(x, axis=2).transpose(0, 2, 1, 3).reshape(b, w * h, c)

        def _seq_block(s, fc1_w, fc1_b, conv_w, conv_b, fc2_w, fc2_b):
            h = jnp.einsum('blc,dc->bld', s, fc1_w) + fc1_b
            hc = h.transpose(0, 2, 1)
            hc = lax.conv_general_dilated(hc, conv_w, window_strides=(1,), padding=[(1, 1)], dimension_numbers=('NCH', 'OIH', 'NCH'), feature_group_count=conv_w.shape[0])
            hc = hc + conv_b[None, :, None]
            h = jax.nn.gelu(hc.transpose(0, 2, 1), approximate=False)
            return jnp.einsum('bld,cd->blc', h, fc2_w) + fc2_b
        b, h, w, c = x.shape
        mu = x.mean(-1, keepdims=True)
        var = ((x - mu) ** 2).mean(-1, keepdims=True)
        xn = (x - mu) / jnp.sqrt(var + EPS) * norm_w + norm_b
        g = xn.mean(-1)[:, None]
        gp = jnp.pad(g, ((0, 0), (0, 0), (1, 1), (1, 1)), mode='reflect')
        grad_h = jnp.abs(gp[:, :, :, 2:] - gp[:, :, :, :-2])
        grad_v = jnp.abs(gp[:, :, 2:, :] - gp[:, :, :-2, :])
        sh = grad_h.mean(axis=(2, 3))
        sv = grad_v.mean(axis=(2, 3))
        scores = jnp.concatenate([sh, sv, (sh + sv) / 2, jnp.abs(sh - sv)], axis=1)
        hid = jax.nn.relu(scores @ sel_w1.T + sel_b1)
        logits = hid @ sel_w2.T + sel_b2
        dir_idx = jnp.argmax(logits, axis=-1)
        outs = []
        for d in range(4):
            seq = _scan_dir(xn, d)
            proc = _seq_block(seq, fc1_w, fc1_b, conv_w, conv_b, fc2_w, fc2_b)
            outs.append(proc.reshape(b, h, w, c))
        stacked = jnp.stack(outs)
        sel = stacked[dir_idx, jnp.arange(b)]
        return x + sel

    def _gn(v, G=32, eps=1e-5):
        B_, H_, W_, C_ = v.shape
        g = v.reshape(B_, H_, W_, G, C_ // G)
        m = jnp.mean(g, axis=(1, 2, 4), keepdims=True)
        s = jnp.var(g, axis=(1, 2, 4), keepdims=True)
        return ((g - m) / jnp.sqrt(s + eps)).reshape(v.shape)

    def _ln_c(v, eps=1e-6):
        m = jnp.mean(v, axis=-1, keepdims=True)
        s = jnp.var(v, axis=-1, keepdims=True)
        return (v - m) / jnp.sqrt(s + eps)

    def _ln_t(v, eps=1e-5):
        m = jnp.mean(v, axis=-1, keepdims=True)
        s = jnp.var(v, axis=-1, keepdims=True)
        return (v - m) / jnp.sqrt(s + eps)

    def _to_tokens(v):
        B_, H_, W_, C_ = v.shape
        return v.reshape(B_, H_ * W_, C_)
    def _from_tokens(t, like):
        return t.reshape(like.shape)

    x = _L0_conv_ref(x, L0_conv_w_q, L0_conv_w_k, L0_conv_w_v, L0_conv_w_o, L0_conv_gamma)
    x = _L1_conv_ref(x, L1_conv_norm_w, L1_conv_norm_b, L1_conv_sel_w1, L1_conv_sel_b1, L1_conv_sel_w2, L1_conv_sel_b2, L1_conv_fc1_w, L1_conv_fc1_b, L1_conv_conv_w, L1_conv_conv_b, L1_conv_fc2_w, L1_conv_fc2_b)
    return x


_drawn_inputs = setup_inputs


def setup_inputs(seed=0):
    import zlib

    import numpy as np

    out = dict(_drawn_inputs(seed))
    spreads = {'L1_conv_norm_w': (1.0, 0.6),
     'L1_conv_norm_b': (0.0, 0.8),
     'L1_conv_sel_b1': (0.0, 0.1),
     'L1_conv_sel_b2': (0.0, 0.1),
     'L1_conv_fc1_b': (0.0, 0.697),
     'L1_conv_conv_b': (0.0, 0.421),
     'L1_conv_fc2_b': (0.0, 0.1)}
    factors = {}
    for name, (base, spread) in spreads.items():
        noise = np.random.default_rng([zlib.crc32(name.encode()), seed]).standard_normal(out[name].shape)
        drawn = base * np.exp(spread * noise) if base else spread * noise
        out[name] = jnp.asarray(drawn.astype(out[name].dtype))
    for name, factor in factors.items():
        out[name] = (out[name] * factor).astype(out[name].dtype)
    return out
```

```python
import concourse.bass as bass
from concourse import mybir
from contextlib import ExitStack

F32 = mybir.dt.float32
F32R = mybir.dt.float32r
I32 = mybir.dt.int32
ALU = mybir.AluOpType
ACT = mybir.ActivationFunctionType
AX = mybir.AxisListType

P = 128
B, HH, WW, C = 8, 64, 64, 192
L = HH * WW
HC = C // 2
D = C // 8
DIN = 2 * C
M1 = DIN // P
CH = 512
NCH = L // CH
TC = CH // P
NT = L // P
G = 32
WARM = 4
RW = CH // WW
NQ = NT // WARM
PS_SLOTS = 8
LN_EPS = 1e-5
OW = C + 1
N_SETUP = 3 + M1 + 2 + 2
N_DIR = 17


def conv_seq_two_layers(nc, x, wqkv, wo, gamma, nwb, nwc, nbc, nb0, sw1, sb1, sw2, sb2,
                        fc1, fc1b, cw, cb, fc2, fc2b, consts, out):
    ctx = ExitStack()
    with ctx:
        def sb(name, shape, dt=F32):
            return ctx.enter_context(nc.sbuf_tensor(name, shape, dt))

        def sem(name):
            return ctx.enter_context(nc.semaphore(name))

        ident = sb("ident", [P, P])
        wdiff = sb("wdiff", [P, P])
        swap = sb("swap", [P, P])
        mean_w = sb("mean_w", [P, P])
        WQKV = sb("WQKV", [HC, 2, 3 * G])
        WO = sb("WO", [P, OW])
        gam = sb("gam", [P, 1])
        NWB = sb("NWB", [P, C])
        NWC = sb("NWC", [HC, 2])
        NBC = sb("NBC", [HC, 2])
        NB0 = sb("NB0", [P, C])
        W1 = sb("W1", [HC, 2, DIN])
        FB1 = sb("FB1", [P, M1])
        CW = sb("CW", [P, M1, 3])
        CB = sb("CB", [P, M1])
        W2 = sb("W2", [P, M1, C])
        B2 = sb("B2", [P, C])
        SW1 = sb("SW1", [1, 4, 16])
        SB1 = sb("SB1", [1, 16])
        SW2 = sb("SW2", [1, 4, 16])
        SB2 = sb("SB2", [1, 4])
        RANK = sb("RANK", [1, 4])
        nbm = sb("nbm", [P, 1])
        XL = sb("XL", [P, 2, TC, C])
        XTC = sb("XTC", [HC, 2, 2, CH])
        QA = sb("QA", [P, L], F32R)
        KA = sb("KA", [P, L], F32R)
        VT = sb("VT", [G, 2, CH])
        V = sb("V", [P, NT, G])
        QC = sb("QC", [P, CH], F32R)
        MP = sb("MP", [P, TC, 4])
        NM = sb("NM", [P, TC])
        PE_ = sb("PE_", [P, PS_SLOTS, CH])
        PVS = sb("PVS", [P, CH])
        XR = sb("XR", [P, TC, C])
        RS = sb("RS", [P, 2])
        X1 = sb("X1", [P, NT, C])
        ST = sb("ST", [P, NT, 6])
        mu = sb("mu", [P, NT])
        dm = sb("dm", [P, NT])
        var = sb("var", [P, NT])
        vs = sb("vs", [P, NT])
        rstd = sb("rstd", [P, NT])
        half = sb("half", [P, NT])
        XN = sb("XN", [P, 2, TC, C])
        GW = sb("GW", [P, 2, TC, C])
        GS = sb("GS", [P, NT])
        GG = sb("GG", [P, NT])
        DV = sb("DV", [P, NT])
        SA = sb("SA", [P, 2])
        XNT = sb("XNT", [HC, 2, L])
        HB = sb("HB", [P, 2, M1, CH + 2])
        T = sb("T", [P, 2, M1, CH])
        SC = sb("SC", [1, 4])
        HID = sb("HID", [1, 16])
        LG = sb("LG", [1, 4, 16])
        LO = sb("LO", [1, 4])
        MX = sb("MX", [1, 1])
        EQ = sb("EQ", [1, 4])
        DF = sb("DF", [1, 1])
        DI = sb("DI", [1, 1], I32)
        PS = ctx.enter_context(nc.psum_tensor("PS", [P, 8, CH], F32))

        wload = sem("wload")
        carried = sem("carried")
        wprep = sem("wprep")
        wb1 = sem("wb1")
        setup = sem("setup")
        xl_loaded = [sem("xl_loaded0"), sem("xl_loaded1")]
        xt_done = sem("xt_done")
        xtc_a = sem("xtc_a")
        xtc_v = sem("xtc_v")
        proj_done = sem("proj_done")
        high_done = sem("high_done")
        low_done = sem("low_done")
        vt_done = sem("vt_done")
        v_ready = sem("v_ready")
        vzero = sem("vzero")
        kone = sem("kone")
        parts_copied = sem("parts_copied")
        qc_loaded = sem("qc_loaded")
        s1_done = sem("s1_done")
        max_done = sem("max_done")
        nm_ready = sem("nm_ready")
        mrow_done = sem("mrow_done")
        qm_ready = sem("qm_ready")
        s2_done = sem("s2_done")
        exp_done = sem("exp_done")
        pv_done = sem("pv_done")
        pvs_ready = sem("pvs_ready")
        xr_loaded = sem("xr_loaded")
        o_done = sem("o_done")
        rs_ready = sem("rs_ready")
        x1_ready = sem("x1_ready")
        bn_done = sem("bn_done")
        stat = sem("stat")
        var_ready = sem("var_ready")
        rstd_ready = sem("rstd_ready")
        newton = sem("newton")
        xn_ready = sem("xn_ready")
        gw_ready = sem("gw_ready")
        gs_ready = sem("gs_ready")
        x1b_ready = sem("x1b_ready")
        xnt_done = sem("xnt_done")
        xnt_a = sem("xnt_a")
        xnt_v = sem("xnt_v")
        g_ready = sem("g_ready")
        diff_done = sem("diff_done")
        sa_ready = sem("sa_ready")
        mean_done = sem("mean_done")
        dir_step = sem("dir_step")
        dir_ready = sem("dir_ready")
        fc1_done = sem("fc1_done")
        h_ready = sem("h_ready")
        halo = sem("halo")
        tap = sem("tap")
        conv_done = sem("conv_done")
        gelu_done = sem("gelu_done")
        fc2_done = sem("fc2_done")
        out_ready = sem("out_ready")
        stored = sem("stored")

        x_t = x.rearrange("b (i p) c -> b p i c", p=P)
        out_t = out.rearrange("b (i p) c -> b p i c", p=P)

        block = ctx.enter_context(nc.Block())

        loads = [
            (ident[:, :], consts[0]), (wdiff[:, :], consts[1]), (swap[:, :], consts[2]),
            (WQKV[:, :, :], wqkv), (WO[:, :], wo), (gam[:, :], gamma), (NWB[:, :], nwb), (NB0[:, :], nb0),
            (NWC[:, :], nwc), (NBC[:, :], nbc), (W1[:, :, :], fc1), (FB1[:, :], fc1b), (CW[:, :, :], cw),
            (CB[:, :], cb), (W2[:, :, :], fc2), (B2[:, :], fc2b), (SW1[:, :, :], sw1), (SB1[:, :], sb1),
            (SW2[:, :, :], sw2), (SB2[:, :], sb2), (RANK[:, :], consts[3, 0:1, 0:4]),
        ]
        NW = len(loads)

        def carry(engine):
            engine.sem_inc(carried, 1)

        @block.sync
        def _(sp):
            for dst, src in loads:
                sp.dma_start(dst, src).then_inc(wload, 16)
            with sp.Fori(0, B) as b:
                with sp.Fori(0, NCH // 2) as i:
                    for u in range(2):
                        sp.wait_ge(xt_done, b * NCH + i * 2 + (u + 1))
                        sp.dma_start(XL[:, u], x_t[bass.ds(b, 1), :, bass.ds(i * (2 * TC) + u * TC, TC), :]
                                     .rearrange("a p i c -> (a p) i c")).then_inc(xl_loaded[u], 16)
                sp.wait_ge(low_done, b * NCH + NCH)
                sp.wait_ge(high_done, b * NCH + NCH)
                carry(sp)
                sp.wait_ge(kone, b + 1)
                for dst, src, g, s in ((QA, QA, 1, 0), (QA, QA, 3, 2), (KA, KA, 2, 0), (KA, KA, 3, 1)):
                    sp.dma_start(dst[g * G:(g + 1) * G, :].bitcast(F32), src[s * G:(s + 1) * G, :].bitcast(F32)).then_inc(parts_copied, 16)
                sp.wait_ge(parts_copied, b * 64 + 64)
                sp.dma_start(QC[:, :].bitcast(F32), QA[:, 0:CH].bitcast(F32)).then_inc(qc_loaded, 16)
                def next_query_chunk(j):
                    sp.wait_ge(s1_done, b * (NCH * 16) + j * 16 + 16)
                    sp.dma_start(QC[:, :].bitcast(F32), QA[:, bass.ds(j * CH + CH, CH)].bitcast(F32)).then_inc(qc_loaded, 16)

                def residual(j):
                    sp.wait_ge(x1_ready, b * (2 * NCH) + j * 2 + 2)
                    sp.dma_start(XR[:, :, :], x_t[bass.ds(b, 1), :, bass.ds(j * TC, TC), :]
                                 .rearrange("a p i c -> (a p) i c")).then_inc(xr_loaded, 16)

                with sp.Fori(0, NCH - 1) as j:
                    next_query_chunk(j)
                    residual(j)
                residual(NCH - 1)
                with sp.Fori(0, NCH) as j:
                    sp.wait_ge(out_ready, b * NCH + j + 2)
                    sp.dma_start(out_t[bass.ds(b, 1), :, bass.ds(j * TC, TC), :]
                                 .rearrange("a p i c -> (a p) i c"),
                                 X1[:, bass.ds(j * TC, TC), :]).then_inc(stored, 16)
            sp.wait_ge(stored, 16 * NCH * B + 16)

        @block.gpsimd
        def _(pool):
            pool.memset(V[:, :, :], 0.0).then_inc(vzero, 1)
            pool.memset(mean_w[:, :], 1.0 / L).then_inc(setup, 1)
            pool.memset(half[:, :], -0.5).then_inc(setup, 1)
            pool.wait_ge(vzero, 1)
            pool.memset(V[:, :, D:D + 1], 1.0).then_inc(setup, 1)
            with pool.Fori(0, B) as b:
                pool.wait_ge(low_done, b * NCH + NCH)
                carry(pool)
                pool.memset(KA[0:1, :].bitcast(F32), 1.0).then_inc(kone, 1)
                pool.wait_ge(var_ready, b + 1)
                pool.tensor_tensor(rstd[:, :], vs[:, :], half[:, :], ALU.pow).then_inc(rstd_ready, 1)
                with pool.Fori(0, NCH // 2) as i:
                    for u in range(2):
                        pool.wait_ge(xn_ready, b * NCH + i * 2 + (u + 1))
                        pool.wait_ge(gs_ready, b * NCH + i * 2 + (u + 1))
                        pool.tensor_tensor(GW[:, u], XN[:, u],
                                           NWB[:, :].unsqueeze(1).broadcast_to([P, TC, C]), ALU.mult).then_inc(gw_ready, 1)
                        xv = X1[:, bass.ds(i * (2 * TC) + u * TC, TC), :]
                        pool.tensor_tensor(xv, xv, B2[:, :].unsqueeze(1).broadcast_to([P, TC, C]),
                                           ALU.add).then_inc(x1b_ready, 1)

        @block.scalar
        def _(act):
            act.wait_ge(wload, 16 * NW)
            act.wait_ge(wb1, 1)
            for m in range(M1):
                ins = nc.scalar.activation(FB1[:, m:m + 1], PS[:, 0, m:m + 1], ACT.Identity, bias=FB1[:, m:m + 1])
                ins.then_inc(setup, 1)
            with act.Fori(0, B) as b:
                with act.Fori(0, NCH // 2) as i:
                    for u in range(2):
                        act.wait_ge(xt_done, b * NCH + i * 2 + (u + 1) + 2)
                        act.wait_ge(proj_done, b * NCH + i * 2 + (u + 1))
                        nc.scalar.activation(XTC[:, u, 0, :], PS[0:HC, 2 * u, :], ACT.Copy).then_inc(xtc_a, 1)
                    for u in range(2):
                        act.wait_ge(proj_done, b * NCH + i * 2 + (u + 1) + 2)
                        sl = bass.ds(i * (2 * CH) + u * CH, CH)
                        nc.scalar.activation(QA[0:G, sl], PS[0:G, 4 + u, :], ACT.Copy)
                        nc.scalar.activation(KA[G:2 * G, sl], PS[G:2 * G, 4 + u, :], ACT.Copy).then_inc(high_done, 1)

                def maximum_row(chunk):
                    act.wait_ge(mrow_done, b * NCH + chunk + 1)
                    nc.scalar.activation(QA[0:1, bass.ds(chunk * CH, CH)], PS[0:1, 7, :], ACT.Copy).then_inc(qm_ready, 1)

                maximum_row(0)
                def attend(j, with_max):
                    for t in range(NT):
                        if t % WARM == 0:
                            act.wait_ge(pv_done, b * (NCH * NQ) + j * NQ + (t // WARM + 1))
                        act.wait_ge(s2_done, b * (NCH * NT) + j * NT + (t + 1))
                        nc.scalar.activation(PE_[:, t % PS_SLOTS, :], PS[:, 4 + t % 2, :], ACT.Exp).then_inc(exp_done, 1)
                    if with_max:
                        maximum_row(j + 1)
                    act.wait_ge(pv_done, b * (NCH * NQ) + j * NQ + (NQ + 2))
                    act.wait_ge(o_done, b * (2 * NCH) + j * 2 + 2)
                    nc.scalar.activation(PVS[:, :], PS[:, 6, :], ACT.Copy).then_inc(pvs_ready, 1)

                with act.Fori(0, NCH - 1) as j:
                    attend(j, True)
                attend(NCH - 1, False)
                with act.Fori(0, NCH // 2) as i:
                    for u in range(2):
                        act.wait_ge(xnt_done, b * NCH + i * 2 + (u + 1) + 2)
                        nc.scalar.activation(XNT[:, 0, bass.ds(i * (2 * CH) + u * CH, CH)],
                                             PS[0:HC, 2 * u, :], ACT.Copy).then_inc(xnt_a, 1)

                def evac_h(c, s):
                    act.wait_ge(fc1_done, b * NCH + c + 1)
                    act.wait_ge(conv_done, b * NCH + c + 1)
                    for m in range(M1):
                        ins = nc.scalar.activation(HB[:, s, m, 1:CH + 1], PS[:, 3 * s + m, :], ACT.Identity,
                                                   bias=FB1[:, m:m + 1])
                    ins.then_inc(h_ready, 1)

                def gelu(c, s):
                    act.wait_ge(conv_done, b * NCH + c + 1 + 2)
                    nc.scalar.activation(T[:, s], T[:, s], ACT.Gelu).then_inc(gelu_done, 1)

                evac_h(0, 0)
                evac_h(1, 1)
                with act.Fori(0, NCH // 2 - 1) as i:
                    for u in range(2):
                        gelu(i * 2 + u, u)
                        evac_h(i * 2 + (u + 2), u)
                gelu(NCH - 2, 0)
                gelu(NCH - 1, 1)

        @block.vector
        def _(dve):
            dve.wait_ge(wload, 16 * NW)
            nc.vector.tensor_scalar(WO[:, 0:C], WO[:, 0:C], gam[:, 0:1], None, ALU.mult).then_inc(setup, 1)
            nc.vector.tensor_reduce(nbm[:, :], NB0[:, :], AX.X, ALU.add).then_inc(wprep, 1)
            dve.wait_ge(wprep, 1)
            nc.vector.tensor_scalar(nbm[:, :], nbm[:, :], 1.0 / C, None, ALU.mult).then_inc(setup, 1)
            dve.wait_ge(wb1, 1)
            for k in range(2):
                nc.vector.tensor_scalar(W1[:, k, :], W1[:, k, :], NWC[:, k:k + 1], None, ALU.mult).then_inc(setup, 1)
            dve.wait_ge(setup, N_SETUP)
            with dve.Fori(0, B) as b:
                with dve.Fori(0, NCH // 2) as i:
                    for u in range(2):
                        dve.wait_ge(xt_done, b * NCH + i * 2 + (u + 1) + 2)
                        dve.wait_ge(proj_done, b * NCH + i * 2 + (u + 1))
                        nc.vector.tensor_copy(XTC[:, u, 1, :], PS[0:HC, 2 * u + 1, :]).then_inc(xtc_v, 1)
                    for u in range(2):
                        sl = bass.ds(i * (2 * CH) + u * CH, CH)
                        dve.wait_ge(proj_done, b * NCH + i * 2 + (u + 1) + 2)
                        nc.vector.tensor_copy(VT[:, u, :], PS[2 * G:3 * G, 4 + u, :])
                        dve.wait_ge(high_done, b * NCH + i * 2 + (u + 1))
                        nc.vector.tensor_tensor(QA[2 * G:3 * G, sl], PS[0:G, 4 + u, :], QA[0:G, sl].bitcast(F32), ALU.subtract)
                        nc.vector.tensor_tensor(KA[0:G, sl], PS[G:2 * G, 4 + u, :], KA[G:2 * G, sl].bitcast(F32),
                                                ALU.subtract).then_inc(low_done, 1)
                    for u in range(2):
                        dve.wait_ge(vt_done, b * NCH + i * 2 + (u + 1))
                        nc.vector.tensor_copy(V[:, bass.ds(i * (2 * TC) + u * TC, TC), 0:D],
                                              PS[:, 6 + u, 0:TC * G].rearrange("p (t e) -> p t e", e=G)[:, :, 0:D]) \
                            .then_inc(v_ready, 1)

                def take_max(chunk, r):
                    dve.wait_ge(s1_done, b * (NCH * 16) + chunk * 16 + (r + 1))
                    nc.vector.tensor_reduce(MP[:, r // 4, r % 4:r % 4 + 1], PS[:, 2 * (r % 2):2 * (r % 2) + 2, :],
                                            AX.XY, ALU.max).then_inc(max_done, 1)

                def join_max(chunk):
                    dve.wait_ge(max_done, b * (NCH * 16) + chunk * 16 + 18)
                    nc.vector.tensor_reduce(NM[:, :], MP[:, :, :], AX.X, ALU.max, negate=True).then_inc(nm_ready, 1)

                def add_layer0(chunk, h):
                    n = b * (2 * NCH) + chunk * 2
                    dve.wait_ge(o_done, n + (h + 1) + 2)
                    ov = PS[:, 7, 0:2 * OW].rearrange("p (t c) -> p t c", c=OW)
                    nc.vector.reciprocal(RS[:, :], ov[:, :, C]).then_inc(rs_ready, 1)
                    if h == 0:
                        dve.wait_ge(xr_loaded, b * (16 * NCH) + chunk * 16 + 16)
                        dve.wait_ge(stored, b * (16 * NCH) + 16)
                    dve.wait_ge(rs_ready, n + (h + 1))
                    for t in range(2):
                        ins = nc.vector.scalar_tensor_tensor(X1[:, bass.ds(chunk * TC + 2 * h + t, 1), :].rearrange("p a c -> p (a c)"),
                                                             ov[:, t, 0:C], RS[:, t:t + 1], XR[:, 2 * h + t, :],
                                                             ALU.mult, ALU.add)
                    ins.then_inc(x1_ready, 1)
                    dve.wait_ge(x1_ready, n + (h + 1) + 2)
                    for t in range(2):
                        tile = chunk * TC + 2 * h + t
                        ins = nc.vector.bn_stats(ST[:, bass.ds(tile, 1), :].rearrange("p a c -> p (a c)"),
                                                 X1[:, bass.ds(tile, 1), :].rearrange("p a c -> p (a c)"))
                    ins.then_inc(bn_done, 1)

                for r in range(16):
                    take_max(0, r)
                join_max(0)
                for r in range(16):
                    take_max(1, r)
                join_max(1)
                with dve.Fori(1, NCH - 1) as j:
                    for r in range(16):
                        take_max(j + 1, r)
                        if r in (7, 11):
                            add_layer0(j - 1, 0 if r == 7 else 1)
                    join_max(j + 1)
                for c in (NCH - 2, NCH - 1):
                    add_layer0(c, 0)
                    add_layer0(c, 1)

                sn = b * 4
                dve.wait_ge(bn_done, b * (2 * NCH) + 2 * NCH)
                nc.vector.tensor_tensor(mu[:, :], ST[:, :, 1], ST[:, :, 4], ALU.add)
                nc.vector.tensor_tensor(dm[:, :], ST[:, :, 1], ST[:, :, 4], ALU.subtract)
                nc.vector.tensor_tensor(var[:, :], ST[:, :, 2], ST[:, :, 5], ALU.add).then_inc(stat, 1)
                dve.wait_ge(stat, sn + 1)
                nc.vector.tensor_scalar(mu[:, :], mu[:, :], 0.5, None, ALU.mult)
                nc.vector.scalar_tensor_tensor(dm[:, :], dm[:, :], 0.25, dm[:, :], ALU.mult, ALU.mult)
                nc.vector.tensor_scalar(var[:, :], var[:, :], 1.0 / C, LN_EPS, ALU.mult, ALU.add).then_inc(stat, 1)
                dve.wait_ge(stat, sn + 2)
                nc.vector.tensor_tensor(vs[:, :], var[:, :], dm[:, :], ALU.add).then_inc(var_ready, 1)
                dve.wait_ge(rstd_ready, b + 1)
                nc.vector.tensor_tensor(dm[:, :], rstd[:, :], rstd[:, :], ALU.mult).then_inc(stat, 1)
                dve.wait_ge(stat, sn + 3)
                nc.vector.scalar_tensor_tensor(dm[:, :], dm[:, :], -0.5, vs[:, :], ALU.mult, ALU.mult).then_inc(stat, 1)
                dve.wait_ge(stat, sn + 4)
                nc.vector.scalar_tensor_tensor(rstd[:, :], dm[:, :], 1.5, rstd[:, :], ALU.add, ALU.mult).then_inc(newton, 1)
                dve.wait_ge(newton, b + 1)
                carry(dve)
                with dve.Fori(0, NCH // 2) as i:
                    for u in range(2):
                        dve.wait_ge(xnt_done, b * NCH + i * 2 + (u + 1))
                        dve.wait_ge(gw_ready, b * NCH + i * 2 + (u + 1))
                        for t in range(TC):
                            tile = i * (2 * TC) + u * TC + t
                            ins = nc.vector.tensor_scalar(XN[:, u, t, :],
                                                          X1[:, bass.ds(tile, 1), :].rearrange("p a c -> p (a c)"),
                                                          mu[:, bass.ds(tile, 1)], rstd[:, bass.ds(tile, 1)],
                                                          ALU.subtract, ALU.mult)
                        ins.then_inc(xn_ready, 1)
                    for u in range(2):
                        dve.wait_ge(xnt_done, b * NCH + i * 2 + (u + 1) + 2)
                        nc.vector.tensor_copy(XNT[:, 1, bass.ds(i * (2 * CH) + u * CH, CH)],
                                              PS[0:HC, 2 * u + 1, :]).then_inc(xnt_v, 1)
                        dve.wait_ge(gw_ready, b * NCH + i * 2 + (u + 1) + 2)
                        nc.vector.tensor_reduce(GS[:, bass.ds(i * (2 * TC) + u * TC, TC)], GW[:, u], AX.X,
                                                ALU.add).then_inc(gs_ready, 1)

                dve.wait_ge(gs_ready, b * NCH + (NCH + 2))
                nc.vector.tensor_scalar(GG[:, :], GS[:, :], 1.0 / C, nbm[:, 0:1], ALU.mult, ALU.add).then_inc(g_ready, 1)
                dve.wait_ge(diff_done, b + 1)
                step = [0]

                def link(ins):
                    step[0] += 1
                    ins.then_inc(dir_step, 1)
                    dve.wait_ge(dir_step, b * N_DIR + step[0])

                link(nc.vector.tensor_copy(DV[:, :], PS[:, 7, NT:2 * NT]))
                link(nc.vector.tensor_tensor(DV[:, 0:NT - 1], PS[:, 7, NT + 1:2 * NT], DV[:, 0:NT - 1], ALU.subtract))
                link(nc.vector.tensor_reduce(SA[:, 0:1], PS[:, 7, 0:NT], AX.X, ALU.add, apply_absolute_value=True))
                link(nc.vector.tensor_reduce(SA[:, 1:2], DV[:, 0:NT - 1], AX.X, ALU.add, apply_absolute_value=True))
                dve.sem_inc(sa_ready, 1)
                dve.wait_ge(mean_done, b + 1)
                link(nc.vector.tensor_copy(SC[:, 0:2], PS[0:1, 7, 0:2]))
                link(nc.vector.tensor_scalar(SC[:, 2:3], SC[:, 0:1], SC[:, 1:2], 0.5, ALU.add, ALU.mult))
                link(nc.vector.tensor_scalar(SC[:, 3:4], SC[:, 0:1], SC[:, 1:2], None, ALU.subtract))
                link(nc.vector.scalar_tensor_tensor(SC[:, 3:4], SC[:, 3:4], -1.0, SC[:, 3:4], ALU.mult, ALU.max))
                for k in range(4):
                    link(nc.vector.scalar_tensor_tensor(HID[:, :], SW1[:, k, :], SC[:, k:k + 1],
                                                        SB1[:, :] if k == 0 else HID[:, :], ALU.mult, ALU.add))
                for k in range(4):
                    ins = nc.vector.scalar_tensor_tensor(LG[:, k, :], HID[:, :], 0.0, SW2[:, k, :], ALU.max, ALU.mult)
                link(ins)
                link(nc.vector.tensor_reduce(LO[:, :], LG[:, :, :], AX.X, ALU.add))
                link(nc.vector.tensor_tensor(LO[:, :], LO[:, :], SB2[:, :], ALU.add))
                link(nc.vector.tensor_reduce(MX[:, :], LO[:, :], AX.X, ALU.max))
                link(nc.vector.scalar_tensor_tensor(EQ[:, :], LO[:, :], MX[:, 0:1], RANK[:, :], ALU.is_equal, ALU.mult))
                assert step[0] == N_DIR, step[0]
                nc.vector.tensor_reduce(DF[:, :], EQ[:, :], AX.X, ALU.add).then_inc(dir_ready, 1)
                dve.wait_ge(dir_ready, b * 2 + 1)
                nc.vector.tensor_copy(DI[:, :], DF[:, :]).then_inc(dir_ready, 1)

                def conv(c, s):
                    dve.wait_ge(fc2_done, b * (2 * NCH) + c * 2 + 2)
                    n = b * (2 * NCH) + c * 2
                    for m in range(M1):
                        ins = nc.vector.tensor_scalar(T[:, s, m, :], HB[:, s, m, 1:CH + 1], CW[:, m, 1:2], CB[:, m:m + 1],
                                                      ALU.mult, ALU.add)
                    ins.then_inc(tap, 1)
                    dve.wait_ge(tap, n + 1)
                    for m in range(M1):
                        ins = nc.vector.scalar_tensor_tensor(T[:, s, m, :], HB[:, s, m, 0:CH], CW[:, m, 0:1], T[:, s, m, :],
                                                             ALU.mult, ALU.add)
                    ins.then_inc(tap, 1)
                    dve.wait_ge(tap, n + 2)
                    for m in range(M1):
                        ins = nc.vector.scalar_tensor_tensor(T[:, s, m, :], HB[:, s, m, 2:CH + 2], CW[:, m, 2:3], T[:, s, m, :],
                                                             ALU.mult, ALU.add)
                    ins.then_inc(conv_done, 1)

                def halos(c, s):
                    dve.wait_ge(h_ready, b * NCH + c + 1)
                    nc.vector.tensor_copy(HB[:, 1 - s, :, CH + 1:CH + 2], HB[:, s, :, 1:2])
                    nc.vector.tensor_copy(HB[:, s, :, 0:1], HB[:, 1 - s, :, CH:CH + 1]).then_inc(halo, 1)
                    dve.wait_ge(halo, b * (NCH + 1) + c + 1)

                def add_layer1(c):
                    for h in range(2):
                        if h == 0:
                            dve.wait_ge(x1b_ready, b * NCH + c + 1)
                        dve.wait_ge(fc2_done, b * (2 * NCH) + c * 2 + (h + 1) + 4)
                        xv = X1[:, bass.ds(c * TC + 2 * h, 2), :]
                        ins = nc.vector.tensor_tensor(xv, PS[:, 6 + h, 0:2 * C].rearrange("p (t c) -> p t c", c=C), xv, ALU.add)
                    ins.then_inc(out_ready, 1)

                dve.wait_ge(h_ready, b * NCH + 1)
                nc.vector.memset(HB[:, 0, :, 0:1], 0.0).then_inc(halo, 1)
                halos(1, 1)
                conv(0, 0)
                with dve.Fori(0, NCH // 2 - 1) as i:
                    for u in range(2):
                        halos(i * 2 + (u + 2), u)
                        conv(i * 2 + (u + 1), 1 - u)
                        add_layer1(i * 2 + u)
                nc.vector.memset(HB[:, 1, :, CH + 1:CH + 2], 0.0).then_inc(halo, 1)
                dve.wait_ge(halo, b * (NCH + 1) + NCH + 1)
                conv(NCH - 1, 1)
                add_layer1(NCH - 2)
                add_layer1(NCH - 1)

        @block.tensor
        def _(pe):
            pe.wait_ge(wload, 16 * NW)
            for m in range(M1):
                for k in range(2):
                    ins = nc.tensor.matmul(PS[:, 0, m:m + 1], W1[:, k, m * P:(m + 1) * P], NBC[:, k:k + 1],
                                           start=(k == 0), stop=(k == 1))
            ins.then_inc(wb1, 1)
            pe.wait_ge(setup, N_SETUP)
            pe.sem_inc(xt_done, 2)
            pe.sem_inc(proj_done, 2)
            pe.sem_inc(x1_ready, 2)
            pe.sem_inc(o_done, 2)
            pe.sem_inc(pv_done, 2)
            pe.sem_inc(exp_done, 2)
            pe.sem_inc(pvs_ready, 1)
            pe.sem_inc(stored, 16)
            pe.sem_inc(gs_ready, 2)
            pe.sem_inc(xnt_done, 2)
            pe.sem_inc(gw_ready, 2)
            pe.sem_inc(conv_done, 2)
            pe.sem_inc(fc2_done, 4)
            pe.sem_inc(xtc_a, 2)
            pe.sem_inc(xtc_v, 2)
            pe.sem_inc(max_done, 2)
            pe.sem_inc(v_ready, 2)
            pe.sem_inc(xnt_a, 2)
            pe.sem_inc(xnt_v, 2)
            pe.sem_inc(out_ready, 1)
            with pe.Fori(0, B) as b:
                with pe.Fori(0, NCH // 2) as i:
                    for u in range(2):
                        pe.wait_ge(xl_loaded[u], b * (8 * NCH) + i * 16 + 16)
                        pe.wait_ge(xtc_a, b * NCH + i * 2 + (u + 1))
                        pe.wait_ge(xtc_v, b * NCH + i * 2 + (u + 1))
                        for t in range(TC):
                            for k in range(2):
                                ins = nc.tensor.transpose(PS[0:HC, 2 * u + k, t * P:(t + 1) * P],
                                                          XL[:, u, t, k * HC:(k + 1) * HC], ident[:, :])
                        ins.then_inc(xt_done, 1)
                    for u in range(2):
                        pe.wait_ge(xtc_a, b * NCH + i * 2 + (u + 1) + 2)
                        pe.wait_ge(xtc_v, b * NCH + i * 2 + (u + 1) + 2)
                        for k in range(2):
                            ins = nc.tensor.matmul(PS[0:3 * G, 4 + u, :], WQKV[:, k, :], XTC[:, u, k, :],
                                                   start=(k == 0), stop=(k == 1))
                        ins.then_inc(proj_done, 1)
                    for u in range(2):
                        pe.wait_ge(low_done, b * NCH + i * 2 + (u + 1))
                        pe.wait_ge(v_ready, b * NCH + i * 2 + (u + 1))
                        for t in range(TC):
                            ins = nc.tensor.matmul(PS[:, 6 + u, t * G:(t + 1) * G], VT[:, u, t * P:(t + 1) * P],
                                                   ident[0:G, 0:G], start=True, stop=True)
                        ins.then_inc(vt_done, 1)

                def s1_matmul(chunk, r, h):
                    if h == 0:
                        pe.wait_ge(max_done, b * (NCH * 16) + chunk * 16 + (r + 1))
                    ins = nc.tensor.matmul(PS[:, 2 * (r % 2) + h, :], QC[:, (r // 4) * P:(r // 4 + 1) * P],
                                           KA[:, (2 * (r % 4) + h) * CH:(2 * (r % 4) + h + 1) * CH], start=True, stop=True)
                    if h == 1:
                        ins.then_inc(s1_done, 1)

                def maximum_row(chunk):
                    pe.wait_ge(nm_ready, b * NCH + chunk + 1)
                    for t in range(TC):
                        ins = nc.tensor.matmul(PS[0:1, 7, t * P:(t + 1) * P], NM[:, t:t + 1], ident[:, :],
                                               start=True, stop=True)
                    ins.then_inc(mrow_done, 1)

                def output_projection(chunk, h):
                    n = b * (2 * NCH) + chunk * 2
                    if h == 0:
                        pe.wait_ge(pvs_ready, b * NCH + chunk + 2)
                    pe.wait_ge(x1_ready, n + (h + 2))
                    for t in range(2):
                        ins = nc.tensor.matmul(PS[:, 7, t * OW:(t + 1) * OW], PVS[:, (2 * h + t) * P:(2 * h + t + 1) * P],
                                               WO[:, :], start=True, stop=True)
                    ins.then_inc(o_done, 1)

                def pv_quad(chunk, q):
                    pe.wait_ge(exp_done, b * (NCH * NT) + chunk * NT + (WARM * q + WARM + 2))
                    if q == 0:
                        pe.wait_ge(pvs_ready, b * NCH + chunk + 1)
                    for g in range(WARM):
                        t = WARM * q + g
                        ins = nc.tensor.matmul(PS[g * G:(g + 1) * G, 6, :], V[:, t, :], PE_[:, t % PS_SLOTS, :],
                                               start=(q == 0), stop=(q == NQ - 1))
                    ins.then_inc(pv_done, 1)

                def attend(j, with_max, with_out):
                    pe.wait_ge(qm_ready, b * NCH + j + 1)
                    if with_max:
                        pe.wait_ge(qc_loaded, b * (16 * NCH) + j * 16 + 32)
                    for q in range(NQ):
                        for g in range(WARM):
                            t = WARM * q + g
                            pe.wait_ge(exp_done, b * (NCH * NT) + j * NT + (t + 1))
                            nc.tensor.matmul(PS[:, 4 + t % 2, :], KA[:, t * P:(t + 1) * P], QA[:, bass.ds(j * CH, CH)],
                                             start=True, stop=True).then_inc(s2_done, 1)
                            if with_max:
                                s1_matmul(j + 1, t // 2, t % 2)
                        if q >= 1:
                            pv_quad(j, q - 1)
                        if with_out and q in (2, 4):
                            output_projection(j - 1, 0 if q == 2 else 1)
                    pv_quad(j, NQ - 1)
                    if with_max:
                        if with_out:
                            pe.wait_ge(x1_ready, b * (2 * NCH) + j * 2 + 2)
                        maximum_row(j + 1)

                pe.wait_ge(parts_copied, b * 64 + 64)
                pe.wait_ge(v_ready, b * NCH + NCH + 2)
                pe.wait_ge(qc_loaded, b * (16 * NCH) + 16)
                for r in range(16):
                    s1_matmul(0, r, 0)
                    s1_matmul(0, r, 1)
                maximum_row(0)
                attend(0, True, False)
                with pe.Fori(1, NCH - 1) as j:
                    attend(j, True, True)
                attend(NCH - 1, False, True)
                output_projection(NCH - 1, 0)
                output_projection(NCH - 1, 1)

                with pe.Fori(0, NCH // 2) as i:
                    for u in range(2):
                        pe.wait_ge(xn_ready, b * NCH + i * 2 + (u + 1))
                        pe.wait_ge(xnt_a, b * NCH + i * 2 + (u + 1))
                        pe.wait_ge(xnt_v, b * NCH + i * 2 + (u + 1))
                        for t in range(TC):
                            for k in range(2):
                                ins = nc.tensor.transpose(PS[0:HC, 2 * u + k, t * P:(t + 1) * P],
                                                          XN[:, u, t, k * HC:(k + 1) * HC], ident[:, :])
                        ins.then_inc(xnt_done, 1)
                pe.wait_ge(g_ready, b + 1)
                pe.wait_ge(x1_ready, b * (2 * NCH) + 2 * NCH + 2)
                nc.tensor.matmul(PS[:, 7, 0:NT], wdiff[:, :], GG[:, :], start=True, stop=True)
                nc.tensor.matmul(PS[:, 7, NT:2 * NT], swap[:, :], GG[:, :], start=True, stop=True).then_inc(diff_done, 1)
                pe.wait_ge(sa_ready, b + 1)
                nc.tensor.matmul(PS[:, 7, 0:2], mean_w[:, :], SA[:, :], start=True, stop=True).then_inc(mean_done, 1)
                pe.wait_ge(xnt_a, b * NCH + NCH + 2)
                pe.wait_ge(xnt_v, b * NCH + NCH + 2)
                pe.wait_ge(dir_ready, b * 2 + 2)
                carry(pe)
                direction = pe.value_load(DI[0:1, 0:1], min_val=0, max_val=15)

                def hidden(c, s):
                    def products(view, place):
                        for m in range(M1):
                            for k in range(2):
                                ins = nc.tensor.matmul(place(m), W1[:, k, m * P:(m + 1) * P], view(k),
                                                       start=(k == 0), stop=(k == 1))
                        ins.then_inc(fc1_done, 1)

                    def bank(m):
                        return PS[:, 3 * s + m, :]

                    def columns(first):
                        return lambda k: XNT[:, k, :].rearrange("p (h w) -> p w h", w=WW)[:, bass.ds(first, RW), :]

                    with pe.If(direction >= 8):
                        products(lambda k: XNT[:, k, bass.ds(c * CH, CH)], bank)
                    with pe.Else():
                        with pe.If(direction >= 2):
                            products(columns(c * RW), bank)
                        with pe.Else():
                            products(columns((NCH - 1 - c) * RW),
                                     lambda m: bank(m).rearrange("p (w h) -> p w h", h=HH)[:, ::-1, :])
                        pe.nop()
                    pe.nop()

                def project_out(c, s):
                    pe.wait_ge(gelu_done, b * NCH + c + 1)
                    pe.wait_ge(out_ready, b * NCH + c + 1)
                    for h in range(2):
                        for t in range(2):
                            for m in range(M1):
                                ins = nc.tensor.matmul(PS[:, 6 + h, t * C:(t + 1) * C],
                                                       T[:, s, m, (2 * h + t) * P:(2 * h + t + 1) * P], W2[:, m, :],
                                                       start=(m == 0), stop=(m == M1 - 1))
                        ins.then_inc(fc2_done, 1)

                hidden(0, 0)
                hidden(1, 1)
                with pe.Fori(0, NCH // 2 - 1) as i:
                    for u in range(2):
                        pe.wait_ge(h_ready, b * NCH + i * 2 + (u + 1))
                        hidden(i * 2 + (u + 2), u)
                        project_out(i * 2 + u, u)
                project_out(NCH - 2, 0)
                project_out(NCH - 1, 1)
                pe.wait_ge(out_ready, b * NCH + NCH + 1)
                pe.wait_ge(h_ready, b * NCH + NCH)


def kernel(**inputs):
    import numpy as np
    import concourse.bacc as bacc
    from concourse.bass_utils import run_bass_kernel_spmd

    a = {k: np.asarray(v) for k, v in inputs.items()}

    def halves(w):
        return np.ascontiguousarray(w.reshape(2, HC, -1).transpose(1, 0, 2))

    def tiles(w):
        return np.ascontiguousarray(w.reshape(M1, P, -1).transpose(1, 0, 2))

    def rows(w):
        return np.ascontiguousarray(np.broadcast_to(w.reshape(1, -1), (P, w.size)))

    f = np.float32
    wqkv = np.zeros((C, 3 * G), f)
    wqkv[:, 1:1 + D] = a["L0_conv_w_q"]
    wqkv[:, G + 1:G + 1 + D] = a["L0_conv_w_k"]
    wqkv[:, 2 * G:2 * G + D] = a["L0_conv_w_v"]
    wo = np.zeros((4, G, OW), f)
    wo[:, 0:D, 0:C] = a["L0_conv_w_o"]
    wo[:, D, C] = 1.0
    consts = np.zeros((4, P, P), f)
    p = np.arange(P)
    inner = p[(p % WW > 0) & (p % WW < WW - 1)]
    consts[0, p, p] = 1.0
    consts[1, inner + 1, inner] = 1.0
    consts[1, inner - 1, inner] = -1.0
    consts[2, p ^ WW, p] = 1.0
    consts[3, 0, 0:4] = (8.0, 4.0, 2.0, 1.0)
    arrays = dict(
        x=a["x"].reshape(B, L, C), wqkv=halves(wqkv), wo=wo.reshape(P, OW), gamma=rows(a["L0_conv_gamma"]),
        nwb=rows(a["L1_conv_norm_w"]), nwc=halves(a["L1_conv_norm_w"])[:, :, 0], nbc=halves(a["L1_conv_norm_b"])[:, :, 0],
        nb0=rows(a["L1_conv_norm_b"]),
        sw1=a["L1_conv_sel_w1"].T.reshape(1, 4, 16), sb1=a["L1_conv_sel_b1"].reshape(1, 16),
        sw2=a["L1_conv_sel_w2"].reshape(1, 4, 16), sb2=a["L1_conv_sel_b2"].reshape(1, 4),
        fc1=halves(a["L1_conv_fc1_w"].T), fc1b=tiles(a["L1_conv_fc1_b"])[:, :, 0], cw=tiles(a["L1_conv_conv_w"].reshape(DIN, 3)),
        cb=tiles(a["L1_conv_conv_b"])[:, :, 0], fc2=tiles(a["L1_conv_fc2_w"].T), fc2b=rows(a["L1_conv_fc2_b"]), consts=consts)
    nc = bacc.Bacc("TRN2", target_bir_lowering=False, num_devices=1)
    given, args = {}, {}
    for name, v in arrays.items():
        v = np.ascontiguousarray(v)
        given[f"in_{name}"] = v
        args[name] = nc.dram_tensor(f"in_{name}", v.shape, mybir.dt.from_np(v.dtype), kind="ExternalInput").ap()
    out = nc.dram_tensor("out_x", (B, L, C), F32, kind="ExternalOutput").ap()
    conv_seq_two_layers(nc, out=out, **args)
    r = run_bass_kernel_spmd(nc, [given], core_ids=[0])
    return r.results[0]["out_x"].reshape(B, HH, WW, C)
```

```python
import concourse.bass as bass
from concourse import mybir
from contextlib import ExitStack

F32 = mybir.dt.float32
F32R = mybir.dt.float32r
I32 = mybir.dt.int32
ALU = mybir.AluOpType
ACT = mybir.ActivationFunctionType
AX = mybir.AxisListType

P = 128
B, HH, WW, C = 8, 64, 64, 192
L = HH * WW
HC = C // 2
D = C // 8
DIN = 2 * C
M1 = DIN // P
CH = 512
NCH = L // CH
TC = CH // P
NT = L // P
G = 32
WARM = 4
RW = CH // WW
NQ = NT // WARM
PS_SLOTS = 8
LN_EPS = 1e-5
OW = C + 1
QT = 4
AHEAD = 5 * QT
PAIRS = NT * QT
N_STEPS = 15
N_SETUP = 7 + M1 + 2 + 2 + 1
N_DIR = 17


def conv_seq_two_layers(nc, x, wqkv, wo, gamma, nwb, nwc, nbc, nb0, sw1, sb1, sw2, sb2,
                        fc1, fc1b, cw, cb, fc2, fc2b, consts, out):
    ctx = ExitStack()
    with ctx:
        def sb(name, shape, dt=F32):
            return ctx.enter_context(nc.sbuf_tensor(name, shape, dt))

        def sem(name):
            return ctx.enter_context(nc.semaphore(name))

        ident = sb("ident", [P, P])
        wdiff = sb("wdiff", [P, P])
        swap = sb("swap", [P, P])
        mean_w = sb("mean_w", [P, P])
        WQKV = sb("WQKV", [HC, 2, 3 * G])
        WO = sb("WO", [P, OW])
        gam = sb("gam", [P, 1])
        NWB = sb("NWB", [P, C])
        NWC = sb("NWC", [HC, 2])
        NBC = sb("NBC", [HC, 2])
        NB0 = sb("NB0", [P, C])
        W1 = sb("W1", [HC, 2, DIN])
        FB1 = sb("FB1", [P, M1])
        CW = sb("CW", [P, M1, 3])
        CB = sb("CB", [P, M1])
        W2 = sb("W2", [P, M1, C])
        B2 = sb("B2", [P, C])
        SW1 = sb("SW1", [1, 4, 16])
        SB1 = sb("SB1", [1, 16])
        SW2 = sb("SW2", [1, 4, 16])
        SB2 = sb("SB2", [1, 4])
        RANK = sb("RANK", [1, 4])
        nbm = sb("nbm", [P, 1])
        XL = sb("XL", [P, 2, TC, C])
        XTC = sb("XTC", [HC, 2, 2, CH])
        QA = sb("QA", [P, L], F32R)
        KA = sb("KA", [P, L], F32R)
        VT = sb("VT", [G, 2, CH])
        V = sb("V", [P, NT, G])
        QC = sb("QC", [P, 5 * P], F32R)
        MP = sb("MP", [P, 5, QT])
        NM = sb("NM", [P, TC])
        PE_ = sb("PE_", [P, PS_SLOTS, CH])
        PVS = sb("PVS", [P, CH])
        XR = sb("XR", [P, TC, C])
        RS = sb("RS", [P, 2])
        X1 = sb("X1", [P, NT, C])
        ST = sb("ST", [P, TC, 6])
        CST = sb("CST", [P, 5, TC])
        TMP = sb("TMP", [P, 6, TC])
        nmr = sb("nmr", [P, TC])
        rstd = sb("rstd", [P, TC])
        XN = sb("XN", [P, TC, C])
        GW = sb("GW", [P, TC, C])
        GS = sb("GS", [P, NT])
        GG = sb("GG", [P, NT])
        DV = sb("DV", [P, NT])
        SA = sb("SA", [P, 2])
        XNT = sb("XNT", [HC, 2, L])
        HB = sb("HB", [P, 2, M1, CH + 2])
        T = sb("T", [P, 2, M1, CH])
        SC = sb("SC", [1, 4])
        HID = sb("HID", [1, 16])
        LG = sb("LG", [1, 4, 16])
        LO = sb("LO", [1, 4])
        MX = sb("MX", [1, 1])
        EQ = sb("EQ", [1, 4])
        DF = sb("DF", [1, 1])
        DI = sb("DI", [1, 1], I32)
        PS = ctx.enter_context(nc.psum_tensor("PS", [P, 8, CH], F32))

        wload = sem("wload")
        carried = sem("carried")
        wprep = sem("wprep")
        wb1 = sem("wb1")
        setup = sem("setup")
        xl_loaded = [sem("xl_loaded0"), sem("xl_loaded1")]
        xt_done = sem("xt_done")
        xtc_a = sem("xtc_a")
        xtc_v = sem("xtc_v")
        proj_done = sem("proj_done")
        high_done = sem("high_done")
        low_done = sem("low_done")
        vt_done = sem("vt_done")
        v_ready = sem("v_ready")
        vzero = sem("vzero")
        parts_copied = [sem(f"parts_copied{i}") for i in range(NCH // 2)]
        q5_loaded = sem("q5_loaded")
        qt_loaded = [sem(f"qt_loaded{k}") for k in range(4)]
        s1_done = sem("s1_done")
        max_done = sem("max_done")
        nm_ready = sem("nm_ready")
        m4_moved = sem("m4_moved")
        mrow_done = sem("mrow_done")
        qm_ready = sem("qm_ready")
        s2_done = sem("s2_done")
        exp_done = sem("exp_done")
        pv_done = sem("pv_done")
        pvs_ready = sem("pvs_ready")
        xr_loaded = sem("xr_loaded")
        o_done = sem("o_done")
        rs_ready = sem("rs_ready")
        x1_ready = sem("x1_ready")
        bn_done = sem("bn_done")
        pool_step = sem("pool_step")
        rstd_ready = sem("rstd_ready")
        xn_ready = sem("xn_ready")
        gw_ready = sem("gw_ready")
        gs_ready = sem("gs_ready")
        x1b_ready = sem("x1b_ready")
        xnt_done = sem("xnt_done")
        xnt_a = sem("xnt_a")
        g_ready = sem("g_ready")
        diff_done = sem("diff_done")
        sa_ready = sem("sa_ready")
        mean_done = sem("mean_done")
        dir_step = sem("dir_step")
        dir_ready = sem("dir_ready")
        fc1_done = sem("fc1_done")
        h_ready = sem("h_ready")
        mid_ready = sem("mid_ready")
        halo = sem("halo")
        tap = sem("tap")
        conv_done = sem("conv_done")
        gelu_done = sem("gelu_done")
        fc2_done = sem("fc2_done")
        out_ready = sem("out_ready")
        stored = sem("stored")

        x_t = x.rearrange("b (i p) c -> b p i c", p=P)
        out_t = out.rearrange("b (i p) c -> b p i c", p=P)

        block = ctx.enter_context(nc.Block())

        loads = [
            (ident[:, :], consts[0]), (wdiff[:, :], consts[1]), (swap[:, :], consts[2]),
            (WQKV[:, :, :], wqkv), (WO[:, :], wo), (gam[:, :], gamma), (NWB[:, :], nwb), (NB0[:, :], nb0),
            (NWC[:, :], nwc), (NBC[:, :], nbc), (W1[:, :, :], fc1), (FB1[:, :], fc1b), (CW[:, :, :], cw),
            (CB[:, :], cb), (W2[:, :, :], fc2), (B2[:, :], fc2b), (SW1[:, :, :], sw1), (SB1[:, :], sb1),
            (SW2[:, :, :], sw2), (SB2[:, :], sb2), (RANK[:, :], consts[3, 0:1, 0:4]),
        ]
        NW = len(loads)

        def score_bank(j, t):
            return (4, 5, 0, 1)[t % 4] if isinstance(j, int) and j == NCH - 1 else 4 + t % 2

        def carry(engine):
            engine.sem_inc(carried, 1)

        @block.sync
        def _(sp):
            for dst, src in loads:
                sp.dma_start(dst, src).then_inc(wload, 16)

            def chunk_of(tensor, b, c):
                return tensor[bass.ds(b, 1), :, bass.ds(c * TC, TC), :].rearrange("a p i c -> (a p) i c")

            def load_x(n, c):
                sp.wait_ge(xt_done, n * NCH + (c + 1))
                carry(sp)
                sp.dma_start(XL[:, c % 2], chunk_of(x_t, n, c)).then_inc(xl_loaded[c % 2], 16)

            def copy_parts(n, i):
                sp.wait_ge(low_done, n * NCH + (2 * i + 4))
                carry(sp)
                cols = slice(i * 2 * CH, (i + 1) * 2 * CH)
                for dst, g, s in ((QA, 1, 0), (QA, 3, 2), (KA, 2, 0), (KA, 3, 1)):
                    sp.dma_start(dst[g * G:(g + 1) * G, cols].bitcast(F32),
                                 dst[s * G:(s + 1) * G, cols].bitcast(F32)).then_inc(parts_copied[i], 16)

            def first_tiles(n):
                sp.wait_ge(parts_copied[0], n * 64 + 64)
                sp.dma_start(QC[:, :].bitcast(F32), QA[:, 0:5 * P].bitcast(F32)).then_inc(q5_loaded, 16)

            def prepare(n):
                for c in range(2, NCH):
                    load_x(n, c)
                    if c % 2 == 0 and c >= 4:
                        copy_parts(n, c // 2 - 2)
                    if c == 5:
                        first_tiles(n)
                for i in (NCH // 2 - 2, NCH // 2 - 1):
                    copy_parts(n, i)

            def load_query(tile, k, tiles=1):
                sp.dma_start(QC[:, k * P:(k + tiles) * P].bitcast(F32),
                             QA[:, bass.ds(tile * P, tiles * P)].bitcast(F32)).then_inc(qt_loaded[k], 16)

            def first_window(b):
                sp.wait_ge(s1_done, b * PAIRS + AHEAD)
                for t in range(5, 9):
                    load_query(t, t % 4)

            def residual(b, j):
                sp.wait_ge(x1_ready, b * (2 * NCH) + j * 2 + 2)
                sp.dma_start(XR[:, :, :], chunk_of(x_t, b, j)).then_inc(xr_loaded, 16)

            def attend(b, j, tiles):
                for k in range(tiles):
                    sp.wait_ge(s1_done, b * PAIRS + j * (4 * QT) + (AHEAD + (k + 1) * QT))
                    load_query(j * 4 + (9 + k), (k + 1) % 4)
                    if k == 1:
                        residual(b, j)
                if tiles < 2:
                    residual(b, j)

            def attention(b):
                with sp.Fori(0, NCH - 3) as j:
                    attend(b, j, 4)
                attend(b, NCH - 3, 3)
                attend(b, NCH - 2, 0)
                attend(b, NCH - 1, 0)

            def store(b, c):
                sp.wait_ge(out_ready, b * NCH + c + 2)
                sp.dma_start(chunk_of(out_t, b, c), X1[:, bass.ds(c * TC, TC), :]).then_inc(stored, 16)

            load_x(0, 0)
            load_x(0, 1)
            prepare(0)
            first_window(0)
            with sp.Fori(0, B - 1) as b:
                attention(b)
                load_x(b + 1, 0)
                load_x(b + 1, 1)
                prepare(b + 1)
                with sp.Fori(0, NCH - 2) as c:
                    store(b, c)
                first_window(b + 1)
                store(b, NCH - 2)
                store(b, NCH - 1)
            attention(B - 1)
            with sp.Fori(0, NCH) as c:
                store(B - 1, c)
            sp.wait_ge(stored, 16 * NCH * B + 16)

        @block.gpsimd
        def _(pool):
            pool.memset(V[:, :, :], 0.0).then_inc(vzero, 1)
            pool.memset(mean_w[:, :], 1.0 / L).then_inc(setup, 1)
            for k, value in enumerate((0.5, 1.0 / C, LN_EPS, -0.5, 1.5)):
                pool.memset(CST[:, k, :], value).then_inc(setup, 1)
            pool.wait_ge(vzero, 1)
            pool.memset(V[:, :, D:D + 1], 1.0).then_inc(setup, 1)
            half, inv_c, eps, neg_half, three_halves = (CST[:, k, :] for k in range(5))

            def statistics(b, c):
                n = b * (NCH * N_STEPS) + c * N_STEPS
                step = [0]

                def op(*parts):
                    for out, x, y, how in parts:
                        step[0] += 1
                        pool.tensor_tensor(out, x, y, how).then_inc(pool_step, 1)
                    pool.wait_ge(pool_step, n + step[0])

                pool.wait_ge(bn_done, b * (2 * NCH) + c * 2 + 2)
                pool.wait_ge(xn_ready, b * NT + c * TC + 1)
                msum, mdiff, vsum, a, y, w = (TMP[:, k, :] for k in range(6))
                op((mdiff, ST[:, :, 1], ST[:, :, 4], ALU.subtract), (vsum, ST[:, :, 2], ST[:, :, 5], ALU.add))
                op((mdiff, mdiff, half, ALU.mult), (vsum, vsum, inv_c, ALU.mult))
                op((mdiff, mdiff, mdiff, ALU.mult), (vsum, vsum, eps, ALU.add))
                op((vsum, vsum, mdiff, ALU.add))
                op((y, vsum, neg_half, ALU.pow), (w, vsum, neg_half, ALU.mult), (msum, ST[:, :, 1], ST[:, :, 4], ALU.add))
                op((a, y, y, ALU.mult), (msum, msum, neg_half, ALU.mult))
                op((a, a, w, ALU.mult))
                op((a, a, three_halves, ALU.add))
                op((rstd[:, :], y, a, ALU.mult))
                assert step[0] == N_STEPS, step[0]
                pool.tensor_tensor(nmr[:, :], msum, rstd[:, :], ALU.mult).then_inc(rstd_ready, 1)

            def weigh(b, c):
                pool.wait_ge(xn_ready, b * NT + c * TC + (TC + 1))
                pool.wait_ge(gs_ready, b * NCH + c + 1)
                pool.tensor_tensor(GW[:, :, :], XN[:, :, :], NWB[:, :].unsqueeze(1).broadcast_to([P, TC, C]),
                                   ALU.mult).then_inc(gw_ready, 1)
                xv = X1[:, bass.ds(c * TC, TC), :]
                pool.tensor_tensor(xv, xv, B2[:, :].unsqueeze(1).broadcast_to([P, TC, C]), ALU.add).then_inc(x1b_ready, 1)

            def attention(b):
                with pool.Fori(0, NCH - 1) as c:
                    statistics(b, c)
                    weigh(b, c)

            with pool.Fori(0, B - 1) as b:
                attention(b)
                statistics(b, NCH - 1)
                weigh(b, NCH - 1)
            attention(B - 1)
            statistics(B - 1, NCH - 1)
            weigh(B - 1, NCH - 1)

        @block.scalar
        def _(act):
            act.wait_ge(wload, 16 * NW)
            act.wait_ge(wb1, 1)
            for m in range(M1):
                nc.scalar.activation(FB1[:, m:m + 1], PS[:, 0, m:m + 1], ACT.Identity,
                                     bias=FB1[:, m:m + 1]).then_inc(setup, 1)

            def copy_xt(n, c):
                act.wait_ge(xt_done, n * NCH + (c + 3))
                act.wait_ge(proj_done, n * NCH + (c + 1))
                nc.scalar.activation(XTC[:, c % 2, 0, :], PS[0:HC, 2 * (c % 2), :], ACT.Copy).then_inc(xtc_a, 1)

            def high_parts(n, c):
                act.wait_ge(proj_done, n * NCH + (c + 3))
                cols = slice(c * CH, (c + 1) * CH)
                nc.scalar.activation(VT[:, c % 2, :], PS[2 * G:3 * G, 4 + c % 2, :], ACT.Copy)
                nc.scalar.activation(QA[0:G, cols], PS[0:G, 4 + c % 2, :], ACT.Copy)
                nc.scalar.activation(KA[G:2 * G, cols], PS[G:2 * G, 4 + c % 2, :], ACT.Copy).then_inc(high_done, 1)

            def copy_sums(b, j):
                act.wait_ge(pv_done, b * (NCH * NQ) + j * NQ + (NQ + 2))
                act.wait_ge(o_done, b * (2 * NCH) + j * 2 + 2)
                nc.scalar.activation(PVS[:, :], PS[:, 6, :], ACT.Copy).then_inc(pvs_ready, 1)

            def copy_xnt(b, c, k):
                act.wait_ge(xnt_done, b * (2 * NCH) + c * 2 + (k + 3))
                nc.scalar.activation(XNT[:, k, bass.ds(c * CH, CH)], PS[0:HC, 7, :], ACT.Copy).then_inc(xnt_a, 1)

            def normalise(b, j, t):
                if t == 0:
                    act.wait_ge(rstd_ready, b * NCH + j + 2)
                    act.wait_ge(xnt_done, b * (2 * NCH) + j * 2 + 2)
                    act.wait_ge(gw_ready, b * NCH + j + 1)
                nc.scalar.activation(XN[:, t, :], X1[:, bass.ds(j * TC + t, 1), :].rearrange("p a c -> p (a c)"),
                                     ACT.Identity, bias=nmr[:, t:t + 1], scale=rstd[:, t:t + 1]).then_inc(xn_ready, 1)

            def turn(b, n):
                if b is not None:
                    copy_sums(b, NCH - 1)
                if n is not None:
                    copy_xt(n, 0)
                for c in range(NCH):
                    if n is not None:
                        if c < NCH - 1:
                            copy_xt(n, c + 1)
                        high_parts(n, c)
                    if b is not None:
                        if c == 3:
                            for t in range(TC):
                                normalise(b, NCH - 1, t)
                        if c in (4, 5):
                            copy_xnt(b, NCH - 1, c - 4)

            def maximum_row(b, j):
                act.wait_ge(mrow_done, b * NCH + j + 1)
                nc.scalar.activation(QA[0:1, bass.ds(j * CH, CH)], PS[0:1, 7, :], ACT.Copy).then_inc(qm_ready, 1)

            def attend(b, j, with_max, with_out):
                for t in range(NT):
                    if t % WARM == 0:
                        act.wait_ge(pv_done, b * (NCH * NQ) + j * NQ + (t // WARM + 1))
                    act.wait_ge(s2_done, b * (NCH * NT) + j * NT + (t + 1))
                    nc.scalar.activation(PE_[:, t % PS_SLOTS, :], PS[:, score_bank(j, t), :], ACT.Exp).then_inc(exp_done, 1)
                    if with_out:
                        if t == 3:
                            copy_sums(b, j - 1)
                        if t in range(17, 17 + TC):
                            normalise(b, j - 1, t - 17)
                        if t in (22, 26):
                            copy_xnt(b, j - 1, 0 if t == 22 else 1)
                    if with_max and t == 30:
                        maximum_row(b, j + 1)

            def attention(b):
                maximum_row(b, 0)
                attend(b, 0, True, False)
                with act.Fori(1, NCH - 1) as j:
                    attend(b, j, True, True)
                attend(b, NCH - 1, False, True)

            def hidden_chunk(b, c, s):
                act.wait_ge(conv_done, b * NCH + c + 1)
                for m in range(M1):
                    act.wait_ge(fc1_done, b * (NCH * M1) + c * M1 + (m + 1))
                    nc.scalar.activation(HB[:, s, m, 1:CH + 1], PS[:, 3 + m, :], ACT.Identity,
                                         bias=FB1[:, m:m + 1]).then_inc(h_ready, 1)

            def middle_tap(b, c, s):
                act.wait_ge(fc2_done, b * (2 * NCH) + c * 2 + 2)
                act.wait_ge(h_ready, b * (NCH * M1) + c * M1 + 2 * M1)
                for m in range(M1):
                    ins = nc.scalar.activation(T[:, s, m, :], HB[:, s, m, 1:CH + 1], ACT.Identity,
                                               bias=CB[:, m:m + 1], scale=CW[:, m, 1:2])
                ins.then_inc(mid_ready, 1)

            def gelu(b, c, s):
                act.wait_ge(conv_done, b * NCH + c + 3)
                nc.scalar.activation(T[:, s], T[:, s], ACT.Gelu).then_inc(gelu_done, 1)

            def feed_forward(b):
                hidden_chunk(b, 0, 0)
                middle_tap(b, 0, 0)
                hidden_chunk(b, 1, 1)
                with act.Fori(0, NCH // 2 - 1) as i:
                    for u in range(2):
                        gelu(b, i * 2 + u, u)
                        middle_tap(b, i * 2 + (u + 1), 1 - u)
                        hidden_chunk(b, i * 2 + (u + 2), u)
                gelu(b, NCH - 2, 0)
                middle_tap(b, NCH - 1, 1)
                gelu(b, NCH - 1, 1)

            turn(None, 0)
            with act.Fori(0, B - 1) as b:
                attention(b)
                turn(b, b + 1)
                feed_forward(b)
            attention(B - 1)
            turn(B - 1, None)
            feed_forward(B - 1)

        @block.vector
        def _(dve):
            dve.wait_ge(wload, 16 * NW)
            nc.vector.tensor_scalar(WO[:, 0:C], WO[:, 0:C], gam[:, 0:1], None, ALU.mult).then_inc(setup, 1)
            nc.vector.tensor_reduce(nbm[:, :], NB0[:, :], AX.X, ALU.add).then_inc(wprep, 1)
            dve.wait_ge(wprep, 1)
            nc.vector.tensor_scalar(nbm[:, :], nbm[:, :], 1.0 / C, None, ALU.mult).then_inc(setup, 1)
            dve.wait_ge(wb1, 1)
            for k in range(2):
                nc.vector.tensor_scalar(W1[:, k, :], W1[:, k, :], NWC[:, k:k + 1], None, ALU.mult).then_inc(setup, 1)
            dve.sem_inc(setup, 1)
            dve.wait_ge(setup, N_SETUP)

            def copy_xt(n, c):
                dve.wait_ge(xt_done, n * NCH + (c + 3))
                dve.wait_ge(proj_done, n * NCH + (c + 1))
                nc.vector.tensor_copy(XTC[:, c % 2, 1, :], PS[0:HC, 2 * (c % 2) + 1, :]).then_inc(xtc_v, 1)

            def low_parts(n, c):
                cols = slice(c * CH, (c + 1) * CH)
                dve.wait_ge(high_done, n * NCH + (c + 1))
                nc.vector.tensor_tensor(QA[2 * G:3 * G, cols], PS[0:G, 4 + c % 2, :], QA[0:G, cols].bitcast(F32),
                                        ALU.subtract)
                nc.vector.scalar_tensor_tensor(KA[0:G, cols], PS[G:2 * G, 4 + c % 2, :], ident[G:2 * G, G:G + 1],
                                               KA[G:2 * G, cols].bitcast(F32), ALU.add, ALU.subtract).then_inc(low_done, 1)

            def copy_v(n, c):
                dve.wait_ge(vt_done, n * NCH + (c + 1))
                nc.vector.tensor_copy(V[:, c * TC:(c + 1) * TC, 0:D],
                                      PS[:, 6, 0:TC * G].rearrange("p (t e) -> p t e", e=G)[:, :, 0:D]).then_inc(v_ready, 1)

            def take_max(b, unit, tile, quarter, bank):
                dve.wait_ge(s1_done, b * PAIRS + unit + 1)
                if isinstance(quarter, int):
                    where = MP[:, tile, quarter:quarter + 1]
                else:
                    where = MP[:, tile, bass.ds(quarter, 1)]
                nc.vector.tensor_reduce(where, PS[:, bank:bank + 2, :], AX.XY, ALU.max).then_inc(max_done, 1)

            def join_max(b, j, units):
                dve.wait_ge(max_done, b * PAIRS + units + 2)
                nc.vector.tensor_reduce(NM[:, :], MP[:, 0:TC, :], AX.X, ALU.max, negate=True).then_inc(nm_ready, 1)

            def add_layer0(b, j, h):
                n = b * (2 * NCH) + j * 2
                if h == 0:
                    dve.wait_ge(xr_loaded, b * (16 * NCH) + j * 16 + 16)
                    dve.wait_ge(stored, b * (16 * NCH) + 16)
                dve.wait_ge(o_done, n + (h + 3))
                ov = PS[:, 7, 0:2 * OW].rearrange("p (t c) -> p t c", c=OW)
                nc.vector.reciprocal(RS[:, :], ov[:, :, C]).then_inc(rs_ready, 1)
                dve.wait_ge(rs_ready, n + (h + 1))
                for t in range(2):
                    ins = nc.vector.scalar_tensor_tensor(
                        X1[:, bass.ds(j * TC + (2 * h + t), 1), :].rearrange("p a c -> p (a c)"),
                        ov[:, t, 0:C], RS[:, t:t + 1], XR[:, 2 * h + t, :], ALU.mult, ALU.add)
                ins.then_inc(x1_ready, 1)

            def token_statistics(b, j, h):
                if h == 0:
                    dve.wait_ge(rstd_ready, b * NCH + j + 1)
                dve.wait_ge(x1_ready, b * (2 * NCH) + j * 2 + (h + 3))
                carry(dve)
                for t in range(2):
                    ins = nc.vector.bn_stats(ST[:, 2 * h + t, :],
                                             X1[:, bass.ds(j * TC + (2 * h + t), 1), :].rearrange("p a c -> p (a c)"))
                ins.then_inc(bn_done, 1)

            def sum_weighted(b, j):
                dve.wait_ge(gw_ready, b * NCH + j + 2)
                nc.vector.tensor_reduce(GS[:, bass.ds(j * TC, TC)], GW[:, :, :], AX.X, ALU.add).then_inc(gs_ready, 1)

            def attend(b, j, units, with_out):
                for u in range(max(units, 1)):
                    if u < units:
                        take_max(b, j * (4 * QT) + (AHEAD + u), (u // QT + 1) % 4, u % QT, 2 * (u % 2))
                    if with_out:
                        if u == 2 or units == 0:
                            add_layer0(b, j - 1, 0)
                        if u == 3 or units == 0:
                            token_statistics(b, j - 1, 0)
                        if u == 4 or units == 0:
                            add_layer0(b, j - 1, 1)
                            token_statistics(b, j - 1, 1)
                        if u == min(14, units - 1) or units == 0:
                            sum_weighted(b, j - 1)
                    if u == 3 * QT - 1:
                        join_max(b, j + 1, j * (4 * QT) + (AHEAD + 3 * QT))
                        dve.wait_ge(nm_ready, b * NCH + j + 2)

            def attention(b):
                attend(b, 0, 4 * QT, False)
                with dve.Fori(1, NCH - 2) as j:
                    attend(b, j, 4 * QT, True)
                attend(b, NCH - 2, 3 * QT, True)
                attend(b, NCH - 1, 0, True)

            step = [0]

            def link(b, ins):
                step[0] += 1
                ins.then_inc(dir_step, 1)
                dve.wait_ge(dir_step, b * N_DIR + step[0])

            def gradient_input(b):
                dve.wait_ge(gs_ready, b * NCH + (NCH + 1))
                nc.vector.tensor_scalar(GG[:, :], GS[:, :], 1.0 / C, nbm[:, 0:1], ALU.mult, ALU.add).then_inc(g_ready, 1)

            def gradient_sums(b):
                step[0] = 0
                dve.wait_ge(diff_done, b + 1)
                link(b, nc.vector.tensor_copy(DV[:, :], PS[:, 7, NT:2 * NT]))
                link(b, nc.vector.tensor_tensor(DV[:, 0:NT - 1], PS[:, 7, NT + 1:2 * NT], DV[:, 0:NT - 1], ALU.subtract))
                link(b, nc.vector.tensor_reduce(SA[:, 0:1], PS[:, 7, 0:NT], AX.X, ALU.add, apply_absolute_value=True))
                link(b, nc.vector.tensor_reduce(SA[:, 1:2], DV[:, 0:NT - 1], AX.X, ALU.add, apply_absolute_value=True))
                dve.sem_inc(sa_ready, 1)

            def choose_direction(b):
                dve.wait_ge(mean_done, b + 1)
                link(b, nc.vector.tensor_copy(SC[:, 0:2], PS[0:1, 7, 0:2]))
                link(b, nc.vector.tensor_scalar(SC[:, 2:3], SC[:, 0:1], SC[:, 1:2], 0.5, ALU.add, ALU.mult))
                link(b, nc.vector.tensor_scalar(SC[:, 3:4], SC[:, 0:1], SC[:, 1:2], None, ALU.subtract))
                link(b, nc.vector.scalar_tensor_tensor(SC[:, 3:4], SC[:, 3:4], -1.0, SC[:, 3:4], ALU.mult, ALU.max))
                for k in range(4):
                    link(b, nc.vector.scalar_tensor_tensor(HID[:, :], SW1[:, k, :], SC[:, k:k + 1],
                                                           SB1[:, :] if k == 0 else HID[:, :], ALU.mult, ALU.add))
                for k in range(4):
                    ins = nc.vector.scalar_tensor_tensor(LG[:, k, :], HID[:, :], 0.0, SW2[:, k, :], ALU.max, ALU.mult)
                link(b, ins)
                link(b, nc.vector.tensor_reduce(LO[:, :], LG[:, :, :], AX.X, ALU.add))
                link(b, nc.vector.tensor_tensor(LO[:, :], LO[:, :], SB2[:, :], ALU.add))
                link(b, nc.vector.tensor_reduce(MX[:, :], LO[:, :], AX.X, ALU.max))
                link(b, nc.vector.scalar_tensor_tensor(EQ[:, :], LO[:, :], MX[:, 0:1], RANK[:, :], ALU.is_equal, ALU.mult))
                assert step[0] == N_DIR, step[0]
                nc.vector.tensor_reduce(DF[:, :], EQ[:, :], AX.X, ALU.add).then_inc(dir_ready, 1)
                dve.wait_ge(dir_ready, b * 2 + 1)
                nc.vector.tensor_copy(DI[:, :], DF[:, :]).then_inc(dir_ready, 1)

            def turn(b, n):
                if n is not None:
                    copy_xt(n, 0)
                for c in range(NCH):
                    if n is not None:
                        if c < NCH - 1:
                            copy_xt(n, c + 1)
                        low_parts(n, c)
                        if c >= 1:
                            copy_v(n, c - 1)
                    if b is not None:
                        if c in (0, 1):
                            add_layer0(b, NCH - 1, c)
                            token_statistics(b, NCH - 1, c)
                        if c == 5:
                            sum_weighted(b, NCH - 1)
                            gradient_input(b)
                        if c == 6:
                            gradient_sums(b)
                        if c == 7:
                            choose_direction(b)
                if n is not None:
                    copy_v(n, NCH - 1)

            def halos(b, c, s):
                dve.wait_ge(h_ready, b * (NCH * M1) + c * M1 + 2 * M1)
                nc.vector.tensor_copy(HB[:, 1 - s, :, CH + 1:CH + 2], HB[:, s, :, 1:2])
                nc.vector.tensor_copy(HB[:, s, :, 0:1], HB[:, 1 - s, :, CH:CH + 1]).then_inc(halo, 1)
                dve.wait_ge(halo, b * (NCH + 1) + c + 1)

            def first_tap(b, c, s):
                dve.wait_ge(mid_ready, b * NCH + c + 1)
                for m in range(M1):
                    ins = nc.vector.scalar_tensor_tensor(T[:, s, m, :], HB[:, s, m, 0:CH], CW[:, m, 0:1], T[:, s, m, :],
                                                         ALU.mult, ALU.add)
                ins.then_inc(tap, 1)

            def last_tap(b, c, s):
                dve.wait_ge(tap, b * NCH + c + 1)
                for m in range(M1):
                    ins = nc.vector.scalar_tensor_tensor(T[:, s, m, :], HB[:, s, m, 2:CH + 2], CW[:, m, 2:3], T[:, s, m, :],
                                                         ALU.mult, ALU.add)
                ins.then_inc(conv_done, 1)

            def add_layer1(b, c):
                dve.wait_ge(x1b_ready, b * NCH + c + 1)
                for h in range(2):
                    dve.wait_ge(fc2_done, b * (2 * NCH) + c * 2 + (h + 5))
                    xv = X1[:, bass.ds(c * TC + 2 * h, 2), :]
                    ins = nc.vector.tensor_tensor(xv, PS[:, 6 + h, 0:2 * C].rearrange("p (t c) -> p t c", c=C), xv, ALU.add)
                ins.then_inc(out_ready, 1)

            def ahead(n, quarter, tiles):
                if n is not None:
                    for k in tiles:
                        take_max(n, quarter * 5 + k, k, quarter, 0)

            def end_ahead(n):
                if n is not None:
                    join_max(n, 0, AHEAD)
                    dve.wait_ge(nm_ready, n * NCH + 1)
                    nc.vector.tensor_copy(MP[:, 0, :], MP[:, 4, :]).then_inc(m4_moved, 1)
                    dve.wait_ge(m4_moved, n + 1)

            def feed_forward(b, n):
                nc.vector.memset(HB[:, 0, :, 0:1], 0.0).then_inc(halo, 1)
                ahead(n, 0, (0, 1, 2, 3, 4))
                halos(b, 1, 1)
                first_tap(b, 0, 0)
                last_tap(b, 0, 0)
                with dve.Fori(0, NCH // 2 - 1) as i:
                    for u in range(2):
                        ahead(n, i + 1, (0,) if u == 0 else (3,))
                        halos(b, i * 2 + (u + 2), u)
                        first_tap(b, i * 2 + (u + 1), 1 - u)
                        ahead(n, i + 1, (1,) if u == 0 else (4,))
                        last_tap(b, i * 2 + (u + 1), 1 - u)
                        ahead(n, i + 1, (2,) if u == 0 else ())
                        add_layer1(b, i * 2 + u)
                end_ahead(n)
                nc.vector.memset(HB[:, 1, :, CH + 1:CH + 2], 0.0).then_inc(halo, 1)
                dve.wait_ge(halo, b * (NCH + 1) + NCH + 1)
                first_tap(b, NCH - 1, 1)
                last_tap(b, NCH - 1, 1)
                add_layer1(b, NCH - 2)
                add_layer1(b, NCH - 1)

            turn(None, 0)
            for q in range(QT):
                ahead(0, q, range(5))
            end_ahead(0)
            with dve.Fori(0, B - 1) as b:
                attention(b)
                turn(b, b + 1)
                feed_forward(b, b + 1)
            attention(B - 1)
            turn(B - 1, None)
            feed_forward(B - 1, None)

        @block.tensor
        def _(pe):
            pe.wait_ge(wload, 16 * NW)
            for m in range(M1):
                for k in range(2):
                    ins = nc.tensor.matmul(PS[:, 0, m:m + 1], W1[:, k, m * P:(m + 1) * P], NBC[:, k:k + 1],
                                           start=(k == 0), stop=(k == 1))
            ins.then_inc(wb1, 1)
            pe.wait_ge(setup, N_SETUP)
            for s, count in ((xt_done, 2), (xtc_a, 2), (xtc_v, 2), (proj_done, 2), (low_done, 2), (v_ready, 1),
                             (max_done, 2), (exp_done, 2), (pv_done, 2), (pvs_ready, 1), (o_done, 2), (x1_ready, 2),
                             (rstd_ready, 1), (xn_ready, 1), (gw_ready, 1), (gs_ready, 1), (xnt_done, 2), (h_ready, M1),
                             (conv_done, 2), (fc2_done, 4), (out_ready, 1), (stored, 16)):
                pe.sem_inc(s, count)

            def transpose_x(n, c):
                u = c % 2
                pe.wait_ge(xl_loaded[u], n * (8 * NCH) + (c // 2 + 1) * 16)
                pe.wait_ge(xtc_a, n * NCH + (c + 1))
                pe.wait_ge(xtc_v, n * NCH + (c + 1))
                for t in range(TC):
                    for k in range(2):
                        ins = nc.tensor.transpose(PS[0:HC, 2 * u + k, t * P:(t + 1) * P],
                                                  XL[:, u, t, k * HC:(k + 1) * HC], ident[:, :])
                ins.then_inc(xt_done, 1)

            def project(n, c):
                u = c % 2
                pe.wait_ge(low_done, n * NCH + (c + 1))
                pe.wait_ge(xtc_a, n * NCH + (c + 3))
                pe.wait_ge(xtc_v, n * NCH + (c + 3))
                for k in range(2):
                    ins = nc.tensor.matmul(PS[0:3 * G, 4 + u, :], WQKV[:, k, :], XTC[:, u, k, :],
                                           start=(k == 0), stop=(k == 1))
                ins.then_inc(proj_done, 1)

            def v_by_key(n, c):
                pe.wait_ge(high_done, n * NCH + (c + 1))
                pe.wait_ge(v_ready, n * NCH + (c + 1))
                for t in range(TC):
                    ins = nc.tensor.matmul(PS[:, 6, t * G:(t + 1) * G], VT[:, c % 2, t * P:(t + 1) * P],
                                           ident[0:G, 0:G], start=True, stop=True)
                ins.then_inc(vt_done, 1)

            def scores_for_max(b, unit, slot, quarter, bank, free):
                pe.wait_ge(max_done, b * PAIRS + unit + free)
                for h in range(2):
                    if isinstance(quarter, int):
                        keys = KA[:, (2 * quarter + h) * CH:(2 * quarter + h + 1) * CH]
                    else:
                        keys = KA[:, bass.ds(quarter * (2 * CH) + h * CH, CH)]
                    ins = nc.tensor.matmul(PS[:, bank + h, :], QC[:, slot * P:(slot + 1) * P], keys, start=True, stop=True)
                ins.then_inc(s1_done, 1)

            def maximum_row(b, j):
                pe.wait_ge(nm_ready, b * NCH + j + 1)
                for t in range(TC):
                    ins = nc.tensor.transpose(PS[0:1, 7, t * P:(t + 1) * P], NM[:, t:t + 1], ident[:, :])
                ins.then_inc(mrow_done, 1)

            def output_projection(b, j, h):
                if h == 0:
                    pe.wait_ge(pvs_ready, b * NCH + j + 2)
                pe.wait_ge(x1_ready, b * (2 * NCH) + j * 2 + (h + 2))
                for t in range(2):
                    ins = nc.tensor.matmul(PS[:, 7, t * OW:(t + 1) * OW], PVS[:, (2 * h + t) * P:(2 * h + t + 1) * P],
                                           WO[:, :], start=True, stop=True)
                ins.then_inc(o_done, 1)

            def transpose_xn(b, j, k):
                if k == 0:
                    pe.wait_ge(x1_ready, b * (2 * NCH) + j * 2 + 4)
                    pe.wait_ge(xn_ready, b * NT + j * TC + (TC + 1))
                else:
                    pe.wait_ge(xnt_a, b * (2 * NCH) + j * 2 + 1)
                for t in range(TC):
                    ins = nc.tensor.transpose(PS[0:HC, 7, t * P:(t + 1) * P], XN[:, t, k * HC:(k + 1) * HC], ident[:, :])
                ins.then_inc(xnt_done, 1)

            def sums_quad(b, j, q):
                pe.wait_ge(exp_done, b * (NCH * NT) + j * NT + (WARM * q + WARM + 2))
                if q == 0:
                    pe.wait_ge(pvs_ready, b * NCH + j + 1)
                for g in range(WARM):
                    t = WARM * q + g
                    ins = nc.tensor.matmul(PS[g * G:(g + 1) * G, 6, :], V[:, t, :], PE_[:, t % PS_SLOTS, :],
                                           start=(q == 0), stop=(q == NQ - 1))
                ins.then_inc(pv_done, 1)

            def attend(b, j, units, with_out):
                pe.wait_ge(qm_ready, b * NCH + j + 1)

                def maxima(u):
                    if u < units:
                        if u % QT == 0:
                            slot = (u // QT + 1) % 4
                            per = 7 if slot else 6
                            pe.wait_ge(qt_loaded[slot], b * (16 * per) + j * 16 + 16)
                        scores_for_max(b, j * (4 * QT) + (AHEAD + u), (u // QT + 1) % 4, u % QT, 2 * (u % 2), 1)

                for q in range(NQ):
                    for g in range(WARM):
                        t = WARM * q + g
                        if units or t < 2:
                            pe.wait_ge(exp_done, b * (NCH * NT) + j * NT + (t + 1))
                        elif t < 4:
                            pe.wait_ge(max_done, b * PAIRS + (PAIRS + 2))
                        else:
                            pe.wait_ge(exp_done, b * (NCH * NT) + j * NT + (t - 1))
                        nc.tensor.matmul(PS[:, score_bank(j, t), :], KA[:, t * P:(t + 1) * P], QA[:, bass.ds(j * CH, CH)],
                                         start=True, stop=True).then_inc(s2_done, 1)
                        if g == 1:
                            maxima(2 * q)
                            if with_out and q in (1, 2):
                                output_projection(b, j - 1, q - 1)
                            if with_out and q in (5, 6):
                                transpose_xn(b, j - 1, q - 5)
                            if q == NQ - 1 and units:
                                if with_out:
                                    pe.wait_ge(xnt_a, b * (2 * NCH) + j * 2)
                                maximum_row(b, j + 1)
                            maxima(2 * q + 1)
                    if q >= 1:
                        sums_quad(b, j, q - 1)
                    elif with_out:
                        sums_quad(b, j - 1, NQ - 1)

            def attention(b):
                pe.wait_ge(v_ready, b * NCH + (NCH + 1))
                maximum_row(b, 0)
                attend(b, 0, 4 * QT, False)
                with pe.Fori(1, NCH - 2) as j:
                    attend(b, j, 4 * QT, True)
                attend(b, NCH - 2, 3 * QT, True)
                attend(b, NCH - 1, 0, True)
                sums_quad(b, NCH - 1, NQ - 1)

            def turn(b, n):
                if n is not None:
                    transpose_x(n, 0)
                for c in range(NCH):
                    if n is not None:
                        if c < NCH - 1:
                            transpose_x(n, c + 1)
                        project(n, c)
                        if c >= 1:
                            v_by_key(n, c - 1)
                    if b is not None:
                        if c in (0, 1):
                            output_projection(b, NCH - 1, c)
                        if c in (4, 5):
                            transpose_xn(b, NCH - 1, c - 4)
                        if c == 6:
                            pe.wait_ge(g_ready, b + 1)
                            pe.wait_ge(xnt_a, b * (2 * NCH) + 2 * NCH)
                            nc.tensor.matmul(PS[:, 7, 0:NT], wdiff[:, :], GG[:, :], start=True, stop=True)
                            nc.tensor.matmul(PS[:, 7, NT:2 * NT], swap[:, :], GG[:, :],
                                             start=True, stop=True).then_inc(diff_done, 1)
                        if c == 7:
                            pe.wait_ge(sa_ready, b + 1)
                            nc.tensor.matmul(PS[:, 7, 0:2], mean_w[:, :], SA[:, :], start=True, stop=True).then_inc(mean_done, 1)
                if n is not None:
                    v_by_key(n, NCH - 1)

            def feed_forward(b, n):
                if n is not None:
                    pe.wait_ge(xtc_a, n * NCH + (NCH + 2))
                    pe.wait_ge(xtc_v, n * NCH + (NCH + 2))
                    pe.wait_ge(low_done, n * NCH + (NCH + 2))
                    pe.wait_ge(v_ready, n * NCH + (NCH + 1))
                pe.wait_ge(dir_ready, b * 2 + 2)
                carry(pe)
                direction = pe.value_load(DI[0:1, 0:1], min_val=0, max_val=15)

                def ahead(quarter, tiles):
                    if n is not None:
                        for k in tiles:
                            scores_for_max(n, quarter * 5 + k, k, quarter, 0, 2)

                def hidden(c):
                    def products(view, place, apart=False):
                        for m in range(M1):
                            pe.wait_ge(h_ready, b * (NCH * M1) + c * M1 + (m + 1))
                            if apart:
                                carry(pe)
                            for k in range(2):
                                ins = nc.tensor.matmul(place(m), W1[:, k, m * P:(m + 1) * P], view(k),
                                                       start=(k == 0), stop=(k == 1))
                            ins.then_inc(fc1_done, 1)

                    def bank(m):
                        return PS[:, 3 + m, :]

                    def columns(first):
                        return lambda k: XNT[:, k, :].rearrange("p (h w) -> p w h", w=WW)[:, bass.ds(first, RW), :]

                    with pe.If(direction >= 8):
                        products(lambda k: XNT[:, k, bass.ds(c * CH, CH)], bank)
                    with pe.Else():
                        with pe.If(direction >= 2):
                            products(columns(c * RW), bank)
                        with pe.Else():
                            products(columns((NCH - 1 - c) * RW),
                                     lambda m: bank(m).rearrange("p (w h) -> p w h", h=HH)[:, ::-1, :], True)
                        pe.nop()
                    pe.nop()

                def project_out(c, s, between=()):
                    pe.wait_ge(gelu_done, b * NCH + c + 1)
                    pe.wait_ge(out_ready, b * NCH + c + 1)
                    for h in range(2):
                        for t in range(2):
                            for m in range(M1):
                                ins = nc.tensor.matmul(PS[:, 6 + h, t * C:(t + 1) * C],
                                                       T[:, s, m, (2 * h + t) * P:(2 * h + t + 1) * P], W2[:, m, :],
                                                       start=(m == 0), stop=(m == M1 - 1))
                        ins.then_inc(fc2_done, 1)
                        if h < len(between):
                            ahead(*between[h])

                hidden(0)
                if n is not None:
                    for copied in parts_copied:
                        pe.wait_ge(copied, n * 64 + 64)
                    pe.wait_ge(q5_loaded, n * 16 + 16)
                ahead(0, (0, 1, 2))
                hidden(1)
                ahead(0, (3, 4))
                with pe.Fori(0, NCH // 2 - 1) as i:
                    hidden(i * 2 + 2)
                    ahead(i + 1, (0,))
                    project_out(i * 2, 0, ((i + 1, (1,)), (i + 1, (2,))))
                    hidden(i * 2 + 3)
                    ahead(i + 1, (3,))
                    project_out(i * 2 + 1, 1, ((i + 1, (4,)),))
                project_out(NCH - 2, 0)
                project_out(NCH - 1, 1)
                pe.wait_ge(out_ready, b * NCH + (NCH + 1))
                pe.wait_ge(h_ready, b * (NCH * M1) + (NCH * M1 + M1))

            turn(None, 0)
            pe.wait_ge(xtc_a, NCH + 2)
            pe.wait_ge(xtc_v, NCH + 2)
            for copied in parts_copied:
                pe.wait_ge(copied, 64)
            pe.wait_ge(q5_loaded, 16)
            for q in range(QT):
                for k in range(5):
                    scores_for_max(0, q * 5 + k, k, q, 0, 2)
            with pe.Fori(0, B - 1) as b:
                attention(b)
                turn(b, b + 1)
                feed_forward(b, b + 1)
            attention(B - 1)
            turn(B - 1, None)
            feed_forward(B - 1, None)


def kernel(**inputs):
    import numpy as np
    import concourse.bacc as bacc
    from concourse.bass_utils import run_bass_kernel_spmd

    a = {k: np.asarray(v) for k, v in inputs.items()}

    def halves(w):
        return np.ascontiguousarray(w.reshape(2, HC, -1).transpose(1, 0, 2))

    def tiles(w):
        return np.ascontiguousarray(w.reshape(M1, P, -1).transpose(1, 0, 2))

    def rows(w):
        return np.ascontiguousarray(np.broadcast_to(w.reshape(1, -1), (P, w.size)))

    f = np.float32
    wqkv = np.zeros((C, 3 * G), f)
    wqkv[:, 1:1 + D] = a["L0_conv_w_q"]
    wqkv[:, G + 1:G + 1 + D] = a["L0_conv_w_k"]
    wqkv[:, 2 * G:2 * G + D] = a["L0_conv_w_v"]
    wo = np.zeros((4, G, OW), f)
    wo[:, 0:D, 0:C] = a["L0_conv_w_o"]
    wo[:, D, C] = 1.0
    consts = np.zeros((4, P, P), f)
    p = np.arange(P)
    inner = p[(p % WW > 0) & (p % WW < WW - 1)]
    consts[0, p, p] = 1.0
    consts[1, inner + 1, inner] = 1.0
    consts[1, inner - 1, inner] = -1.0
    consts[2, p ^ WW, p] = 1.0
    consts[3, 0, 0:4] = (8.0, 4.0, 2.0, 1.0)
    arrays = dict(
        x=a["x"].reshape(B, L, C), wqkv=halves(wqkv), wo=wo.reshape(P, OW), gamma=rows(a["L0_conv_gamma"]),
        nwb=rows(a["L1_conv_norm_w"]), nwc=halves(a["L1_conv_norm_w"])[:, :, 0], nbc=halves(a["L1_conv_norm_b"])[:, :, 0],
        nb0=rows(a["L1_conv_norm_b"]),
        sw1=a["L1_conv_sel_w1"].T.reshape(1, 4, 16), sb1=a["L1_conv_sel_b1"].reshape(1, 16),
        sw2=a["L1_conv_sel_w2"].reshape(1, 4, 16), sb2=a["L1_conv_sel_b2"].reshape(1, 4),
        fc1=halves(a["L1_conv_fc1_w"].T), fc1b=tiles(a["L1_conv_fc1_b"])[:, :, 0], cw=tiles(a["L1_conv_conv_w"].reshape(DIN, 3)),
        cb=tiles(a["L1_conv_conv_b"])[:, :, 0], fc2=tiles(a["L1_conv_fc2_w"].T), fc2b=rows(a["L1_conv_fc2_b"]), consts=consts)
    nc = bacc.Bacc("TRN2", target_bir_lowering=False, num_devices=1)
    given, args = {}, {}
    for name, v in arrays.items():
        v = np.ascontiguousarray(v)
        given[f"in_{name}"] = v
        args[name] = nc.dram_tensor(f"in_{name}", v.shape, mybir.dt.from_np(v.dtype), kind="ExternalInput").ap()
    out = nc.dram_tensor("out_x", (B, L, C), F32, kind="ExternalOutput").ap()
    conv_seq_two_layers(nc, out=out, **args)
    r = run_bass_kernel_spmd(nc, [given], core_ids=[0])
    return r.results[0]["out_x"].reshape(B, HH, WW, C)
```

```python
import concourse.bass as bass
from concourse import mybir
from contextlib import ExitStack

F32 = mybir.dt.float32
F32R = mybir.dt.float32r
I32 = mybir.dt.int32
ALU = mybir.AluOpType
ACT = mybir.ActivationFunctionType
AX = mybir.AxisListType

P = 128
B, HH, WW, C = 8, 64, 64, 192
L = HH * WW
HC = C // 2
D = C // 8
DIN = 2 * C
M1 = DIN // P
CH = 512
NCH = L // CH
TC = CH // P
NT = L // P
G = 32
WARM = 4
RW = CH // WW
NQ = NT // WARM
PS_SLOTS = 8
LN_EPS = 1e-5
OW = C + 1
QT = 4
FIRST = TC + 2
AHEAD = FIRST * QT
PAIRS = NT * QT
N_STEPS = 15
N_SETUP = 7 + M1 + 2 + 2 + 1
N_DIR = 17


def conv_seq_two_layers(nc, x, wqkv, wo, gamma, nwb, nwc, nbc, nb0, sw1, sb1, sw2, sb2,
                        fc1, fc1b, cw, cb, fc2, fc2b, consts, out):
    ctx = ExitStack()
    with ctx:
        def sb(name, shape, dt=F32):
            return ctx.enter_context(nc.sbuf_tensor(name, shape, dt))

        def sem(name):
            return ctx.enter_context(nc.semaphore(name))

        ident = sb("ident", [P, P])
        wdiff = sb("wdiff", [P, P])
        swap = sb("swap", [P, P])
        mean_w = sb("mean_w", [P, P])
        WQKV = sb("WQKV", [HC, 2, 3 * G])
        WO = sb("WO", [P, OW])
        gam = sb("gam", [P, 1])
        NWB = sb("NWB", [P, C])
        NWC = sb("NWC", [HC, 2])
        NBC = sb("NBC", [HC, 2])
        NB0 = sb("NB0", [P, C])
        W1 = sb("W1", [HC, 2, DIN])
        FB1 = sb("FB1", [P, M1])
        CW = sb("CW", [P, M1, 3])
        CB = sb("CB", [P, M1])
        W2 = sb("W2", [P, M1, C])
        B2 = sb("B2", [P, C])
        SW1 = sb("SW1", [1, 4, 16])
        SB1 = sb("SB1", [1, 16])
        SW2 = sb("SW2", [1, 4, 16])
        SB2 = sb("SB2", [1, 4])
        RANK = sb("RANK", [1, 4])
        nbm = sb("nbm", [P, 1])
        XL = sb("XL", [P, 2, TC, C])
        XTC = sb("XTC", [HC, 2, 2, CH])
        QA = sb("QA", [P, L], F32R)
        KA = sb("KA", [P, L], F32R)
        VT = sb("VT", [G, 2, CH])
        V = sb("V", [P, NT, G])
        QC = sb("QC", [P, FIRST * P], F32R)
        MP = sb("MP", [P, FIRST, QT])
        NM = sb("NM", [P, TC])
        PE_ = sb("PE_", [P, PS_SLOTS, CH])
        PVS = sb("PVS", [P, CH])
        XR = sb("XR", [P, TC, C])
        RS = sb("RS", [P, 2])
        X1 = sb("X1", [P, NT, C])
        ST = sb("ST", [P, TC, 6])
        CST = sb("CST", [P, 5, TC])
        TMP = sb("TMP", [P, 6, TC])
        nmr = sb("nmr", [P, TC])
        rstd = sb("rstd", [P, TC])
        XN = sb("XN", [P, TC, C])
        GW = sb("GW", [P, TC, C])
        GS = sb("GS", [P, NT])
        GG = sb("GG", [P, NT])
        DV = sb("DV", [P, NT])
        SA = sb("SA", [P, 2])
        XNT = sb("XNT", [HC, 2, L])
        HB = sb("HB", [P, 2, M1, CH + 2])
        T = sb("T", [P, 2, M1, CH])
        SC = sb("SC", [1, 4])
        HID = sb("HID", [1, 16])
        LG = sb("LG", [1, 4, 16])
        LO = sb("LO", [1, 4])
        MX = sb("MX", [1, 1])
        EQ = sb("EQ", [1, 4])
        DF = sb("DF", [1, 1])
        DI = sb("DI", [1, 1], I32)
        PS = ctx.enter_context(nc.psum_tensor("PS", [P, 8, CH], F32))

        wload = sem("wload")
        carried = sem("carried")
        wprep = sem("wprep")
        wb1 = sem("wb1")
        setup = sem("setup")
        xl_loaded = [sem("xl_loaded0"), sem("xl_loaded1")]
        xt_done = sem("xt_done")
        xtc_a = sem("xtc_a")
        xtc_v = sem("xtc_v")
        proj_done = sem("proj_done")
        high_done = sem("high_done")
        low_done = sem("low_done")
        vt_done = sem("vt_done")
        v_ready = sem("v_ready")
        vzero = sem("vzero")
        parts_copied = [sem(f"parts_copied{i}") for i in range(NCH // 2)]
        first_loaded = sem("first_loaded")
        qt_loaded = [sem(f"qt_loaded{k}") for k in range(4)]
        s1_done = sem("s1_done")
        max_done = sem("max_done")
        nm_ready = sem("nm_ready")
        early_moved = sem("early_moved")
        mrow_done = sem("mrow_done")
        qm_ready = sem("qm_ready")
        s2_done = sem("s2_done")
        exp_done = sem("exp_done")
        pv_done = sem("pv_done")
        pvs_ready = sem("pvs_ready")
        xr_loaded = sem("xr_loaded")
        o_done = sem("o_done")
        rs_ready = sem("rs_ready")
        x1_ready = sem("x1_ready")
        bn_done = sem("bn_done")
        pool_step = sem("pool_step")
        rstd_ready = sem("rstd_ready")
        xn_ready = sem("xn_ready")
        gw_ready = sem("gw_ready")
        gs_ready = sem("gs_ready")
        x1b_ready = sem("x1b_ready")
        xnt_done = sem("xnt_done")
        xnt_a = sem("xnt_a")
        g_ready = sem("g_ready")
        diff_done = sem("diff_done")
        sa_ready = sem("sa_ready")
        mean_done = sem("mean_done")
        scores_taken = sem("scores_taken")
        dir_step = sem("dir_step")
        dir_ready = sem("dir_ready")
        fc1_done = sem("fc1_done")
        h_ready = sem("h_ready")
        mid_ready = sem("mid_ready")
        halo = sem("halo")
        tap = sem("tap")
        conv_done = sem("conv_done")
        gelu_done = sem("gelu_done")
        fc2_done = sem("fc2_done")
        out_ready = sem("out_ready")
        stored = sem("stored")

        x_t = x.rearrange("b (i p) c -> b p i c", p=P)
        out_t = out.rearrange("b (i p) c -> b p i c", p=P)

        block = ctx.enter_context(nc.Block())

        loads = [
            (ident[:, :], consts[0]), (wdiff[:, :], consts[1]), (swap[:, :], consts[2]),
            (WQKV[:, :, :], wqkv), (WO[:, :], wo), (gam[:, :], gamma), (NWB[:, :], nwb), (NB0[:, :], nb0),
            (NWC[:, :], nwc), (NBC[:, :], nbc), (W1[:, :, :], fc1), (FB1[:, :], fc1b), (CW[:, :, :], cw),
            (CB[:, :], cb), (W2[:, :, :], fc2), (B2[:, :], fc2b), (SW1[:, :, :], sw1), (SB1[:, :], sb1),
            (SW2[:, :, :], sw2), (SB2[:, :], sb2), (RANK[:, :], consts[3, 0:1, 0:4]),
        ]
        NW = len(loads)

        def score_bank(j, t):
            return (4, 5, 0, 1)[t % 4] if isinstance(j, int) and j == NCH - 1 else 4 + t % 2

        def row_bank(j):
            return 3 if isinstance(j, int) and j == 0 else 7

        def hidden_bank(m):
            return 3 + (M1 - 1 - m)

        def ahead_bank(quarter, k):
            return (0, 2, 0, 6, 0, 6)[k] if isinstance(quarter, int) and quarter == 0 else 0

        def carry(engine):
            engine.sem_inc(carried, 1)

        @block.sync
        def _(sp):
            def chunk_of(tensor, b, c):
                return tensor[bass.ds(b, 1), :, bass.ds(c * TC, TC), :].rearrange("a p i c -> (a p) i c")

            for c in range(2):
                sp.dma_start(XL[:, c], chunk_of(x_t, 0, c)).then_inc(xl_loaded[c], 16)
            for dst, src in loads:
                sp.dma_start(dst, src).then_inc(wload, 16)

            def load_x(n, c):
                sp.wait_ge(xt_done, n * NCH + (c + 1))
                carry(sp)
                sp.dma_start(XL[:, c % 2], chunk_of(x_t, n, c)).then_inc(xl_loaded[c % 2], 16)

            def copy_parts(n, i):
                sp.wait_ge(low_done, n * NCH + (2 * i + 4))
                carry(sp)
                cols = slice(i * 2 * CH, (i + 1) * 2 * CH)
                for dst, g, s in ((QA, 1, 0), (QA, 3, 2), (KA, 2, 0), (KA, 3, 1)):
                    sp.dma_start(dst[g * G:(g + 1) * G, cols].bitcast(F32),
                                 dst[s * G:(s + 1) * G, cols].bitcast(F32)).then_inc(parts_copied[i], 16)

            def first_tiles(n):
                sp.wait_ge(parts_copied[0], n * 64 + 64)
                sp.dma_start(QC[:, :].bitcast(F32), QA[:, 0:FIRST * P].bitcast(F32)).then_inc(first_loaded, 16)

            def prepare(n):
                for c in range(2, NCH):
                    load_x(n, c)
                    if c == 5:
                        copy_parts(n, 0)
                    if c == 6:
                        first_tiles(n)
                for i in range(1, NCH // 2):
                    copy_parts(n, i)

            def load_query(tile, k, tiles=1):
                sp.dma_start(QC[:, k * P:(k + tiles) * P].bitcast(F32),
                             QA[:, bass.ds(tile * P, tiles * P)].bitcast(F32)).then_inc(qt_loaded[k], 16)

            def first_window(b):
                sp.wait_ge(s1_done, b * PAIRS + AHEAD)
                for t in range(FIRST, FIRST + 4):
                    load_query(t, t % 4)

            def residual(b, j):
                sp.wait_ge(x1_ready, b * (2 * NCH) + j * 2 + 2)
                sp.dma_start(XR[:, :, :], chunk_of(x_t, b, j)).then_inc(xr_loaded, 16)

            def attend(b, j, tiles):
                for k in range(tiles):
                    sp.wait_ge(s1_done, b * PAIRS + j * (4 * QT) + (AHEAD + (k + 1) * QT))
                    load_query(j * 4 + (FIRST + 4 + k), (FIRST + k) % 4)
                    if k == 1:
                        residual(b, j)
                if tiles < 2:
                    residual(b, j)

            def attention(b):
                with sp.Fori(0, NCH - 3) as j:
                    attend(b, j, 4)
                attend(b, NCH - 3, 2)
                attend(b, NCH - 2, 0)
                attend(b, NCH - 1, 0)

            def store(b, c):
                sp.wait_ge(out_ready, b * NCH + c + 2)
                sp.dma_start(chunk_of(out_t, b, c), X1[:, bass.ds(c * TC, TC), :]).then_inc(stored, 16)

            prepare(0)
            first_window(0)
            with sp.Fori(0, B - 1) as b:
                attention(b)
                load_x(b + 1, 0)
                load_x(b + 1, 1)
                prepare(b + 1)
                with sp.Fori(0, NCH - 2) as c:
                    store(b, c)
                first_window(b + 1)
                store(b, NCH - 2)
                store(b, NCH - 1)
            attention(B - 1)
            with sp.Fori(0, NCH) as c:
                store(B - 1, c)
            sp.wait_ge(stored, 16 * NCH * B + 16)

        @block.gpsimd
        def _(pool):
            pool.memset(V[:, :, :], 0.0).then_inc(vzero, 1)
            pool.memset(mean_w[:, :], 1.0 / L).then_inc(setup, 1)
            for k, value in enumerate((0.5, 1.0 / C, LN_EPS, -0.5, 1.5)):
                pool.memset(CST[:, k, :], value).then_inc(setup, 1)
            pool.wait_ge(vzero, 1)
            pool.memset(V[:, :, D:D + 1], 1.0).then_inc(setup, 1)
            half, inv_c, eps, neg_half, three_halves = (CST[:, k, :] for k in range(5))

            def statistics(b, c):
                n = b * (NCH * N_STEPS) + c * N_STEPS
                step = [0]

                def op(*parts):
                    for out, x, y, how in parts:
                        step[0] += 1
                        pool.tensor_tensor(out, x, y, how).then_inc(pool_step, 1)
                    pool.wait_ge(pool_step, n + step[0])

                pool.wait_ge(bn_done, b * (2 * NCH) + c * 2 + 2)
                pool.wait_ge(xn_ready, b * NT + c * TC + 1)
                msum, mdiff, vsum, a, y, w = (TMP[:, k, :] for k in range(6))
                op((mdiff, ST[:, :, 1], ST[:, :, 4], ALU.subtract), (vsum, ST[:, :, 2], ST[:, :, 5], ALU.add))
                op((mdiff, mdiff, half, ALU.mult), (vsum, vsum, inv_c, ALU.mult))
                op((mdiff, mdiff, mdiff, ALU.mult), (vsum, vsum, eps, ALU.add))
                op((vsum, vsum, mdiff, ALU.add))
                op((y, vsum, neg_half, ALU.pow), (w, vsum, neg_half, ALU.mult), (msum, ST[:, :, 1], ST[:, :, 4], ALU.add))
                op((a, y, y, ALU.mult), (msum, msum, neg_half, ALU.mult))
                op((a, a, w, ALU.mult))
                op((a, a, three_halves, ALU.add))
                op((rstd[:, :], y, a, ALU.mult))
                assert step[0] == N_STEPS, step[0]
                pool.tensor_tensor(nmr[:, :], msum, rstd[:, :], ALU.mult).then_inc(rstd_ready, 1)

            def weigh(b, c):
                pool.wait_ge(xn_ready, b * NT + c * TC + (TC + 1))
                pool.wait_ge(gs_ready, b * NCH + c + 1)
                pool.tensor_tensor(GW[:, :, :], XN[:, :, :], NWB[:, :].unsqueeze(1).broadcast_to([P, TC, C]),
                                   ALU.mult).then_inc(gw_ready, 1)
                xv = X1[:, bass.ds(c * TC, TC), :]
                pool.tensor_tensor(xv, xv, B2[:, :].unsqueeze(1).broadcast_to([P, TC, C]), ALU.add).then_inc(x1b_ready, 1)

            def attention(b):
                with pool.Fori(0, NCH - 1) as c:
                    statistics(b, c)
                    weigh(b, c)

            with pool.Fori(0, B - 1) as b:
                attention(b)
                statistics(b, NCH - 1)
                weigh(b, NCH - 1)
            attention(B - 1)
            statistics(B - 1, NCH - 1)
            weigh(B - 1, NCH - 1)

        @block.scalar
        def _(act):
            act.wait_ge(wload, 16 * NW)
            act.wait_ge(wb1, 1)
            for m in range(M1):
                nc.scalar.activation(FB1[:, m:m + 1], PS[:, 0, m:m + 1], ACT.Identity,
                                     bias=FB1[:, m:m + 1]).then_inc(setup, 1)

            def copy_xt(n, c):
                act.wait_ge(xt_done, n * NCH + (c + 3))
                act.wait_ge(proj_done, n * NCH + (c + 1))
                nc.scalar.activation(XTC[:, c % 2, 0, :], PS[0:HC, 2 * (c % 2), :], ACT.Copy).then_inc(xtc_a, 1)

            def high_parts(n, c):
                act.wait_ge(proj_done, n * NCH + (c + 3))
                cols = slice(c * CH, (c + 1) * CH)
                nc.scalar.activation(VT[:, c % 2, :], PS[2 * G:3 * G, 4 + c % 2, :], ACT.Copy)
                nc.scalar.activation(QA[0:G, cols], PS[0:G, 4 + c % 2, :], ACT.Copy)
                nc.scalar.activation(KA[G:2 * G, cols], PS[G:2 * G, 4 + c % 2, :], ACT.Copy).then_inc(high_done, 1)

            def copy_sums(b, j):
                act.wait_ge(pv_done, b * (NCH * NQ) + j * NQ + (NQ + 2))
                act.wait_ge(o_done, b * (2 * NCH) + j * 2 + 2)
                nc.scalar.activation(PVS[:, :], PS[:, 6, :], ACT.Copy).then_inc(pvs_ready, 1)

            def copy_xnt(b, c, k):
                act.wait_ge(xnt_done, b * (2 * NCH) + c * 2 + (k + 3))
                nc.scalar.activation(XNT[:, k, :].rearrange("p (w h) -> p w h", h=HH)[:, :, bass.ds(c * RW, RW)],
                                     PS[0:HC, 7, :].rearrange("p (h w) -> p w h", w=WW), ACT.Copy).then_inc(xnt_a, 1)

            def normalise(b, j, t):
                if t == 0:
                    act.wait_ge(rstd_ready, b * NCH + j + 2)
                    act.wait_ge(xnt_done, b * (2 * NCH) + j * 2 + 2)
                    act.wait_ge(gw_ready, b * NCH + j + 1)
                nc.scalar.activation(XN[:, t, :], X1[:, bass.ds(j * TC + t, 1), :].rearrange("p a c -> p (a c)"),
                                     ACT.Identity, bias=nmr[:, t:t + 1], scale=rstd[:, t:t + 1]).then_inc(xn_ready, 1)

            def turn(b, n):
                if b is not None:
                    copy_sums(b, NCH - 1)
                if n is not None:
                    copy_xt(n, 0)
                for c in range(NCH):
                    if n is not None:
                        if c < NCH - 1:
                            copy_xt(n, c + 1)
                    if b is not None and c == 4:
                        for t in range(TC // 2, TC):
                            normalise(b, NCH - 1, t)
                    if n is not None:
                        high_parts(n, c)
                    if b is not None:
                        if c == 3:
                            for t in range(TC // 2):
                                normalise(b, NCH - 1, t)
                        if c == 4:
                            copy_xnt(b, NCH - 1, 0)
                if b is not None:
                    copy_xnt(b, NCH - 1, 1)

            def maximum_row(b, j):
                act.wait_ge(mrow_done, b * NCH + j + 1)
                nc.scalar.activation(QA[0:1, bass.ds(j * CH, CH)], PS[0:1, row_bank(j), :], ACT.Copy).then_inc(qm_ready, 1)

            def attend(b, j, with_max, with_out):
                for t in range(NT):
                    if t % WARM == 0:
                        act.wait_ge(pv_done, b * (NCH * NQ) + j * NQ + (t // WARM + 1))
                    act.wait_ge(s2_done, b * (NCH * NT) + j * NT + (t + 1))
                    nc.scalar.activation(PE_[:, t % PS_SLOTS, :], PS[:, score_bank(j, t), :], ACT.Exp).then_inc(exp_done, 1)
                    if with_out:
                        if t == 3:
                            copy_sums(b, j - 1)
                        if t in (19, 21, 23, 25):
                            normalise(b, j - 1, (t - 19) // 2)
                        if t in (27, 31):
                            copy_xnt(b, j - 1, 0 if t == 27 else 1)
                    if with_max and t == 17:
                        maximum_row(b, j + 1)

            def attention(b):
                maximum_row(b, 0)
                attend(b, 0, True, False)
                with act.Fori(1, NCH - 1) as j:
                    attend(b, j, True, True)
                attend(b, NCH - 1, False, True)

            def hidden_chunk(b, c, s):
                act.wait_ge(conv_done, b * NCH + c + 1)
                for m in range(M1):
                    act.wait_ge(fc1_done, b * (NCH * M1) + c * M1 + (m + 1))
                    nc.scalar.activation(HB[:, s, m, 1:CH + 1], PS[:, hidden_bank(m), :], ACT.Identity,
                                         bias=FB1[:, m:m + 1]).then_inc(h_ready, 1)

            def middle_tap(b, c, s):
                act.wait_ge(fc2_done, b * (2 * NCH) + c * 2 + 2)
                act.wait_ge(h_ready, b * (NCH * M1) + c * M1 + 2 * M1)
                for m in range(M1):
                    ins = nc.scalar.activation(T[:, s, m, :], HB[:, s, m, 1:CH + 1], ACT.Identity,
                                               bias=CB[:, m:m + 1], scale=CW[:, m, 1:2])
                ins.then_inc(mid_ready, 1)

            def gelu(b, c, s):
                act.wait_ge(conv_done, b * NCH + c + 3)
                nc.scalar.activation(T[:, s], T[:, s], ACT.Gelu).then_inc(gelu_done, 1)

            def feed_forward(b):
                hidden_chunk(b, 0, 0)
                middle_tap(b, 0, 0)
                hidden_chunk(b, 1, 1)
                with act.Fori(0, NCH // 2 - 1) as i:
                    for u in range(2):
                        middle_tap(b, i * 2 + (u + 1), 1 - u)
                        gelu(b, i * 2 + u, u)
                        hidden_chunk(b, i * 2 + (u + 2), u)
                middle_tap(b, NCH - 1, 1)
                gelu(b, NCH - 2, 0)
                gelu(b, NCH - 1, 1)

            turn(None, 0)
            with act.Fori(0, B - 1) as b:
                attention(b)
                turn(b, b + 1)
                feed_forward(b)
            attention(B - 1)
            turn(B - 1, None)
            feed_forward(B - 1)

        @block.vector
        def _(dve):
            dve.wait_ge(wload, 16 * NW)
            nc.vector.tensor_scalar(WO[:, 0:C], WO[:, 0:C], gam[:, 0:1], None, ALU.mult).then_inc(setup, 1)
            nc.vector.tensor_reduce(nbm[:, :], NB0[:, :], AX.X, ALU.add).then_inc(wprep, 1)
            dve.wait_ge(wprep, 1)
            nc.vector.tensor_scalar(nbm[:, :], nbm[:, :], 1.0 / C, None, ALU.mult).then_inc(setup, 1)
            dve.wait_ge(wb1, 1)
            for k in range(2):
                nc.vector.tensor_scalar(W1[:, k, :], W1[:, k, :], NWC[:, k:k + 1], None, ALU.mult).then_inc(setup, 1)
            dve.sem_inc(setup, 1)
            dve.wait_ge(setup, N_SETUP)

            def copy_xt(n, c):
                dve.wait_ge(xt_done, n * NCH + (c + 3))
                dve.wait_ge(proj_done, n * NCH + (c + 1))
                nc.vector.tensor_copy(XTC[:, c % 2, 1, :], PS[0:HC, 2 * (c % 2) + 1, :]).then_inc(xtc_v, 1)

            def low_parts(n, c):
                cols = slice(c * CH, (c + 1) * CH)
                dve.wait_ge(high_done, n * NCH + (c + 1))
                nc.vector.tensor_tensor(QA[2 * G:3 * G, cols], PS[0:G, 4 + c % 2, :], QA[0:G, cols].bitcast(F32),
                                        ALU.subtract)
                nc.vector.scalar_tensor_tensor(KA[0:G, cols], PS[G:2 * G, 4 + c % 2, :], ident[G:2 * G, G:G + 1],
                                               KA[G:2 * G, cols].bitcast(F32), ALU.add, ALU.subtract).then_inc(low_done, 1)

            def copy_v(n, c):
                dve.wait_ge(vt_done, n * NCH + (c + 1))
                nc.vector.tensor_copy(V[:, c * TC:(c + 1) * TC, 0:D],
                                      PS[:, 6, 0:TC * G].rearrange("p (t e) -> p t e", e=G)[:, :, 0:D]).then_inc(v_ready, 1)

            def take_max(b, unit, tile, quarter, bank):
                dve.wait_ge(s1_done, b * PAIRS + unit + 1)
                if isinstance(quarter, int):
                    where = MP[:, tile, quarter:quarter + 1]
                else:
                    where = MP[:, tile, bass.ds(quarter, 1)]
                nc.vector.tensor_reduce(where, PS[:, bank:bank + 2, :], AX.XY, ALU.max).then_inc(max_done, 1)

            def join_max(b, j, units):
                dve.wait_ge(max_done, b * PAIRS + units + 2)
                nc.vector.tensor_reduce(NM[:, :], MP[:, 0:TC, :], AX.X, ALU.max, negate=True).then_inc(nm_ready, 1)

            def add_layer0(b, j, h):
                n = b * (2 * NCH) + j * 2
                if h == 0:
                    dve.wait_ge(xr_loaded, b * (16 * NCH) + j * 16 + 16)
                    dve.wait_ge(stored, b * (16 * NCH) + 16)
                dve.wait_ge(o_done, n + (h + 3))
                ov = PS[:, 7, 0:2 * OW].rearrange("p (t c) -> p t c", c=OW)
                nc.vector.reciprocal(RS[:, :], ov[:, :, C]).then_inc(rs_ready, 1)
                dve.wait_ge(rs_ready, n + (h + 1))
                for t in range(2):
                    ins = nc.vector.scalar_tensor_tensor(
                        X1[:, bass.ds(j * TC + (2 * h + t), 1), :].rearrange("p a c -> p (a c)"),
                        ov[:, t, 0:C], RS[:, t:t + 1], XR[:, 2 * h + t, :], ALU.mult, ALU.add)
                ins.then_inc(x1_ready, 1)

            def token_statistics(b, j, h):
                if h == 0:
                    dve.wait_ge(rstd_ready, b * NCH + j + 1)
                dve.wait_ge(x1_ready, b * (2 * NCH) + j * 2 + (h + 3))
                carry(dve)
                for t in range(2):
                    ins = nc.vector.bn_stats(ST[:, 2 * h + t, :],
                                             X1[:, bass.ds(j * TC + (2 * h + t), 1), :].rearrange("p a c -> p (a c)"))
                ins.then_inc(bn_done, 1)

            def sum_weighted(b, j):
                dve.wait_ge(gw_ready, b * NCH + j + 2)
                nc.vector.tensor_reduce(GS[:, bass.ds(j * TC, TC)], GW[:, :, :], AX.X, ALU.add).then_inc(gs_ready, 1)

            def attend(b, j, units, with_out):
                for u in range(max(units, 1)):
                    if u < units:
                        take_max(b, j * (4 * QT) + (AHEAD + u), (u // QT + FIRST) % 4, u % QT, 2 * (u % 2))
                    if with_out:
                        if u == 2 or units == 0:
                            add_layer0(b, j - 1, 0)
                        if u == 3 or units == 0:
                            token_statistics(b, j - 1, 0)
                        if u == 4 or units == 0:
                            add_layer0(b, j - 1, 1)
                        if u == 5 or units == 0:
                            token_statistics(b, j - 1, 1)
                    if u == 2 * QT - 1:
                        join_max(b, j + 1, j * (4 * QT) + (AHEAD + 2 * QT))
                        dve.wait_ge(nm_ready, b * NCH + j + 2)
                    if with_out and (u == min(14, units - 1) or units == 0):
                        sum_weighted(b, j - 1)

            def attention(b):
                attend(b, 0, 4 * QT, False)
                with dve.Fori(1, NCH - 2) as j:
                    attend(b, j, 4 * QT, True)
                attend(b, NCH - 2, 2 * QT, True)
                attend(b, NCH - 1, 0, True)

            step = [0]

            def link(b, ins):
                step[0] += 1
                ins.then_inc(dir_step, 1)
                dve.wait_ge(dir_step, b * N_DIR + step[0])

            def gradient_input(b):
                dve.wait_ge(gs_ready, b * NCH + (NCH + 1))
                nc.vector.tensor_scalar(GG[:, :], GS[:, :], 1.0 / C, nbm[:, 0:1], ALU.mult, ALU.add).then_inc(g_ready, 1)

            def gradient_sums(b):
                step[0] = 0
                dve.wait_ge(diff_done, b + 1)
                link(b, nc.vector.tensor_copy(DV[:, :], PS[:, 7, NT:2 * NT]))
                link(b, nc.vector.tensor_tensor(DV[:, 0:NT - 1], PS[:, 7, NT + 1:2 * NT], DV[:, 0:NT - 1], ALU.subtract))
                link(b, nc.vector.tensor_reduce(SA[:, 0:1], PS[:, 7, 0:NT], AX.X, ALU.add, apply_absolute_value=True))
                link(b, nc.vector.tensor_reduce(SA[:, 1:2], DV[:, 0:NT - 1], AX.X, ALU.add, apply_absolute_value=True))
                dve.sem_inc(sa_ready, 1)

            def direction_scores(b):
                dve.wait_ge(mean_done, b + 1)
                link(b, nc.vector.tensor_copy(SC[:, 0:2], PS[0:1, 7, 0:2]))
                dve.sem_inc(scores_taken, 1)
                link(b, nc.vector.tensor_scalar(SC[:, 2:3], SC[:, 0:1], SC[:, 1:2], 0.5, ALU.add, ALU.mult))
                link(b, nc.vector.tensor_scalar(SC[:, 3:4], SC[:, 0:1], SC[:, 1:2], None, ALU.subtract))
                link(b, nc.vector.scalar_tensor_tensor(SC[:, 3:4], SC[:, 3:4], -1.0, SC[:, 3:4], ALU.mult, ALU.max))
                for k in range(4):
                    link(b, nc.vector.scalar_tensor_tensor(HID[:, :], SW1[:, k, :], SC[:, k:k + 1],
                                                           SB1[:, :] if k == 0 else HID[:, :], ALU.mult, ALU.add))

            def choose_direction(b):
                for k in range(4):
                    ins = nc.vector.scalar_tensor_tensor(LG[:, k, :], HID[:, :], 0.0, SW2[:, k, :], ALU.max, ALU.mult)
                link(b, ins)
                link(b, nc.vector.tensor_reduce(LO[:, :], LG[:, :, :], AX.X, ALU.add))
                link(b, nc.vector.tensor_tensor(LO[:, :], LO[:, :], SB2[:, :], ALU.add))
                link(b, nc.vector.tensor_reduce(MX[:, :], LO[:, :], AX.X, ALU.max))
                link(b, nc.vector.scalar_tensor_tensor(EQ[:, :], LO[:, :], MX[:, 0:1], RANK[:, :], ALU.is_equal, ALU.mult))
                assert step[0] == N_DIR, step[0]
                nc.vector.tensor_reduce(DF[:, :], EQ[:, :], AX.X, ALU.add).then_inc(dir_ready, 1)
                dve.wait_ge(dir_ready, b * 2 + 1)
                nc.vector.tensor_copy(DI[:, :], DF[:, :]).then_inc(dir_ready, 1)

            def turn(b, n):
                if n is not None:
                    copy_xt(n, 0)
                for c in range(NCH):
                    if n is not None:
                        if c < NCH - 1:
                            copy_xt(n, c + 1)
                    if b is not None and c == 6:
                        direction_scores(b)
                    if b is not None and c == 7:
                        choose_direction(b)
                    if n is not None:
                        low_parts(n, c)
                        if c >= 1:
                            copy_v(n, c - 1)
                    if b is not None:
                        if c in (0, 1):
                            add_layer0(b, NCH - 1, c)
                            token_statistics(b, NCH - 1, c)
                        if c == 4:
                            sum_weighted(b, NCH - 1)
                            gradient_input(b)
                        if c == 5:
                            gradient_sums(b)
                if n is not None:
                    copy_v(n, NCH - 1)

            def halos(b, c, s):
                dve.wait_ge(h_ready, b * (NCH * M1) + c * M1 + 2 * M1)
                nc.vector.tensor_copy(HB[:, 1 - s, :, CH + 1:CH + 2], HB[:, s, :, 1:2])
                nc.vector.tensor_copy(HB[:, s, :, 0:1], HB[:, 1 - s, :, CH:CH + 1]).then_inc(halo, 1)
                dve.wait_ge(halo, b * (NCH + 1) + c + 1)

            def first_tap(b, c, s):
                dve.wait_ge(mid_ready, b * NCH + c + 1)
                for m in range(M1):
                    ins = nc.vector.scalar_tensor_tensor(T[:, s, m, :], HB[:, s, m, 0:CH], CW[:, m, 0:1], T[:, s, m, :],
                                                         ALU.mult, ALU.add)
                ins.then_inc(tap, 1)

            def last_tap(b, c, s):
                dve.wait_ge(tap, b * NCH + c + 1)
                for m in range(M1):
                    ins = nc.vector.scalar_tensor_tensor(T[:, s, m, :], HB[:, s, m, 2:CH + 2], CW[:, m, 2:3], T[:, s, m, :],
                                                         ALU.mult, ALU.add)
                ins.then_inc(conv_done, 1)

            def add_layer1(b, c):
                dve.wait_ge(x1b_ready, b * NCH + c + 1)
                for h in range(2):
                    dve.wait_ge(fc2_done, b * (2 * NCH) + c * 2 + (h + 5))
                    xv = X1[:, bass.ds(c * TC + 2 * h, 2), :]
                    ins = nc.vector.tensor_tensor(xv, PS[:, 6 + h, 0:2 * C].rearrange("p (t c) -> p t c", c=C), xv, ALU.add)
                ins.then_inc(out_ready, 1)

            def ahead(n, quarter, tiles):
                if n is not None:
                    for k in tiles:
                        take_max(n, quarter * FIRST + k, k, quarter, ahead_bank(quarter, k))

            def end_ahead(n):
                if n is not None:
                    join_max(n, 0, AHEAD)
                    dve.wait_ge(nm_ready, n * NCH + 1)
                    nc.vector.tensor_copy(MP[:, 0:FIRST - TC, :], MP[:, TC:FIRST, :]).then_inc(early_moved, 1)
                    dve.wait_ge(early_moved, n + 1)

            def feed_forward(b, n):
                nc.vector.memset(HB[:, 0, :, 0:1], 0.0).then_inc(halo, 1)
                ahead(n, 0, (0, 1, 2, 3))
                dve.wait_ge(halo, b * (NCH + 1) + 1)
                first_tap(b, 0, 0)
                halos(b, 1, 1)
                last_tap(b, 0, 0)
                ahead(n, 0, (4, 5))
                first_tap(b, 1, 1)
                with dve.Fori(0, NCH // 2 - 1) as i:
                    for u in range(2):
                        ahead(n, i + 1, (3 * u, 3 * u + 1))
                        halos(b, i * 2 + (u + 2), u)
                        last_tap(b, i * 2 + (u + 1), 1 - u)
                        ahead(n, i + 1, (3 * u + 2,))
                        add_layer1(b, i * 2 + u)
                        first_tap(b, i * 2 + (u + 2), u)
                end_ahead(n)
                nc.vector.memset(HB[:, 1, :, CH + 1:CH + 2], 0.0).then_inc(halo, 1)
                dve.wait_ge(halo, b * (NCH + 1) + NCH + 1)
                last_tap(b, NCH - 1, 1)
                add_layer1(b, NCH - 2)
                add_layer1(b, NCH - 1)

            turn(None, 0)
            for unit in range(AHEAD):
                take_max(0, unit, unit % FIRST, unit // FIRST, 2 * (unit % 2))
            end_ahead(0)
            with dve.Fori(0, B - 1) as b:
                attention(b)
                turn(b, b + 1)
                feed_forward(b, b + 1)
            attention(B - 1)
            turn(B - 1, None)
            feed_forward(B - 1, None)

        @block.tensor
        def _(pe):
            pe.wait_ge(wload, 16 * NW)
            for m in range(M1):
                for k in range(2):
                    ins = nc.tensor.matmul(PS[:, 0, m:m + 1], W1[:, k, m * P:(m + 1) * P], NBC[:, k:k + 1],
                                           start=(k == 0), stop=(k == 1))
            ins.then_inc(wb1, 1)
            pe.wait_ge(setup, N_SETUP)
            for s, count in ((xt_done, 2), (xtc_a, 2), (xtc_v, 2), (proj_done, 2), (low_done, 2), (v_ready, 1),
                             (max_done, 2), (exp_done, 2), (pv_done, 2), (pvs_ready, 1), (o_done, 2), (x1_ready, 2),
                             (rstd_ready, 1), (xn_ready, 1), (gw_ready, 1), (gs_ready, 1), (xnt_done, 2), (h_ready, M1),
                             (conv_done, 2), (fc2_done, 4), (out_ready, 1), (stored, 16)):
                pe.sem_inc(s, count)

            def transpose_x(n, c):
                u = c % 2
                pe.wait_ge(xl_loaded[u], n * (8 * NCH) + (c // 2 + 1) * 16)
                pe.wait_ge(xtc_a, n * NCH + (c + 1))
                pe.wait_ge(xtc_v, n * NCH + (c + 1))
                for t in range(TC):
                    for k in range(2):
                        ins = nc.tensor.transpose(PS[0:HC, 2 * u + k, t * P:(t + 1) * P],
                                                  XL[:, u, t, k * HC:(k + 1) * HC], ident[:, :])
                ins.then_inc(xt_done, 1)

            def project(n, c):
                u = c % 2
                pe.wait_ge(low_done, n * NCH + (c + 1))
                pe.wait_ge(xtc_a, n * NCH + (c + 3))
                pe.wait_ge(xtc_v, n * NCH + (c + 3))
                for k in range(2):
                    ins = nc.tensor.matmul(PS[0:3 * G, 4 + u, :], WQKV[:, k, :], XTC[:, u, k, :],
                                           start=(k == 0), stop=(k == 1))
                ins.then_inc(proj_done, 1)

            def v_by_key(n, c):
                pe.wait_ge(high_done, n * NCH + (c + 1))
                pe.wait_ge(v_ready, n * NCH + (c + 1))
                carry(pe)
                for t in range(TC):
                    ins = nc.tensor.transpose(PS[:, 6, t * G:(t + 1) * G], VT[:, c % 2, t * P:(t + 1) * P],
                                              ident[0:G, 0:G])
                ins.then_inc(vt_done, 1)

            def scores_for_max(b, unit, slot, quarter, bank, free):
                pe.wait_ge(max_done, b * PAIRS + unit + free)
                for h in range(2):
                    if isinstance(quarter, int):
                        keys = KA[:, (2 * quarter + h) * CH:(2 * quarter + h + 1) * CH]
                    else:
                        keys = KA[:, bass.ds(quarter * (2 * CH) + h * CH, CH)]
                    ins = nc.tensor.matmul(PS[:, bank + h, :], QC[:, slot * P:(slot + 1) * P], keys, start=True, stop=True)
                ins.then_inc(s1_done, 1)

            def scores_ahead(n, quarter, tiles):
                for k in tiles:
                    scores_for_max(n, quarter * FIRST + k, k, quarter, ahead_bank(quarter, k),
                                   1 if isinstance(quarter, int) and quarter == 0 else 2)

            def maximum_row(b, j):
                pe.wait_ge(nm_ready, b * NCH + j + 1)
                for t in range(TC):
                    ins = nc.tensor.transpose(PS[0:1, row_bank(j), t * P:(t + 1) * P], NM[:, t:t + 1], ident[:, :])
                ins.then_inc(mrow_done, 1)

            def output_projection(b, j, h):
                if h == 0:
                    pe.wait_ge(pvs_ready, b * NCH + j + 2)
                    pe.wait_ge(xnt_a, b * (2 * NCH) + j * 2)
                pe.wait_ge(x1_ready, b * (2 * NCH) + j * 2 + (h + 2))
                for t in range(2):
                    ins = nc.tensor.matmul(PS[:, 7, t * OW:(t + 1) * OW], PVS[:, (2 * h + t) * P:(2 * h + t + 1) * P],
                                           WO[:, :], start=True, stop=True)
                ins.then_inc(o_done, 1)

            def transpose_xn(b, j, k):
                if k == 0:
                    pe.wait_ge(x1_ready, b * (2 * NCH) + j * 2 + 4)
                    pe.wait_ge(qm_ready, b * NCH + (NCH if isinstance(j, int) else j + 3))
                    pe.wait_ge(xn_ready, b * NT + j * TC + (TC + 1))
                else:
                    pe.wait_ge(xnt_a, b * (2 * NCH) + j * 2 + 1)
                for t in range(TC):
                    ins = nc.tensor.transpose(PS[0:HC, 7, t * P:(t + 1) * P], XN[:, t, k * HC:(k + 1) * HC], ident[:, :])
                ins.then_inc(xnt_done, 1)

            def sums_quad(b, j, q):
                pe.wait_ge(exp_done, b * (NCH * NT) + j * NT + (WARM * q + WARM + 2))
                if q == 0:
                    pe.wait_ge(pvs_ready, b * NCH + j + 1)
                    if isinstance(j, int) and j == 0:
                        pe.wait_ge(out_ready, b * NCH + 1)
                for g in range(WARM):
                    t = WARM * q + g
                    ins = nc.tensor.matmul(PS[g * G:(g + 1) * G, 6, :], V[:, t, :], PE_[:, t % PS_SLOTS, :],
                                           start=(q == 0), stop=(q == NQ - 1))
                ins.then_inc(pv_done, 1)

            def attend(b, j, units, with_out):
                pe.wait_ge(qm_ready, b * NCH + j + 1)

                def maxima(u):
                    if u < units:
                        slot = (u // QT + FIRST) % 4
                        if u % QT == 0:
                            pe.wait_ge(qt_loaded[slot], b * (16 * len(range(FIRST + u // QT, NT, 4))) + j * 16 + 16)
                        scores_for_max(b, j * (4 * QT) + (AHEAD + u), slot, u % QT, 2 * (u % 2), 1)

                for q in range(NQ):
                    for g in range(WARM):
                        t = WARM * q + g
                        if units or t < 2:
                            pe.wait_ge(exp_done, b * (NCH * NT) + j * NT + (t + 1))
                        elif t < 4:
                            pe.wait_ge(max_done, b * PAIRS + (PAIRS + 2))
                        else:
                            pe.wait_ge(exp_done, b * (NCH * NT) + j * NT + (t - 1))
                        nc.tensor.matmul(PS[:, score_bank(j, t), :], KA[:, t * P:(t + 1) * P], QA[:, bass.ds(j * CH, CH)],
                                         start=True, stop=True).then_inc(s2_done, 1)
                        if g == 1:
                            maxima(2 * q)
                            if with_out and q in (1, 2):
                                output_projection(b, j - 1, q - 1)
                            if q == 4:
                                maxima(2 * q + 1)
                            if q == 4 and units:
                                if with_out:
                                    pe.wait_ge(x1_ready, b * (2 * NCH) + j * 2 + 2)
                                maximum_row(b, j + 1)
                            if with_out and q == 7:
                                transpose_xn(b, j - 1, 1)
                            if q != 4:
                                maxima(2 * q + 1)
                    if with_out and q == 6:
                        transpose_xn(b, j - 1, 0)
                    if q >= 1:
                        sums_quad(b, j, q - 1)
                    elif with_out:
                        sums_quad(b, j - 1, NQ - 1)

            def attention(b):
                pe.wait_ge(v_ready, b * NCH + (NCH + 1))
                attend(b, 0, 4 * QT, False)
                with pe.Fori(1, NCH - 2) as j:
                    attend(b, j, 4 * QT, True)
                attend(b, NCH - 2, 2 * QT, True)
                attend(b, NCH - 1, 0, True)
                sums_quad(b, NCH - 1, NQ - 1)

            def turn(b, n):
                if n is not None:
                    transpose_x(n, 0)
                for c in range(NCH):
                    if n is not None:
                        if c < NCH - 1:
                            transpose_x(n, c + 1)
                        project(n, c)
                        if c >= 1:
                            v_by_key(n, c - 1)
                    if b is not None:
                        if c in (0, 1):
                            output_projection(b, NCH - 1, c)
                        if c == 4:
                            transpose_xn(b, NCH - 1, 0)
                        if c == 5:
                            pe.wait_ge(g_ready, b + 1)
                            pe.wait_ge(xnt_a, b * (2 * NCH) + 2 * NCH - 1)
                            nc.tensor.matmul(PS[:, 7, 0:NT], wdiff[:, :], GG[:, :], start=True, stop=True)
                            nc.tensor.matmul(PS[:, 7, NT:2 * NT], swap[:, :], GG[:, :],
                                             start=True, stop=True).then_inc(diff_done, 1)
                        if c == 6:
                            pe.wait_ge(sa_ready, b + 1)
                            nc.tensor.matmul(PS[:, 7, 0:2], mean_w[:, :], SA[:, :], start=True, stop=True).then_inc(mean_done, 1)
                if b is not None:
                    pe.wait_ge(scores_taken, b + 1)
                    transpose_xn(b, NCH - 1, 1)

            def feed_forward(b, n):
                if n is not None:
                    pe.wait_ge(xtc_a, n * NCH + (NCH + 2))
                    pe.wait_ge(xtc_v, n * NCH + (NCH + 2))
                    pe.wait_ge(parts_copied[0], n * 64 + 64)
                    pe.wait_ge(first_loaded, n * 16 + 16)
                    scores_ahead(n, 0, (0, 1))
                    v_by_key(n, NCH - 1)
                    pe.wait_ge(low_done, n * NCH + (NCH + 2))
                    pe.wait_ge(v_ready, n * NCH + (NCH + 1))
                pe.wait_ge(xnt_a, b * (2 * NCH) + 2 * NCH)
                pe.wait_ge(dir_ready, b * 2 + 2)
                carry(pe)
                direction = pe.value_load(DI[0:1, 0:1], min_val=0, max_val=15)

                def ahead(quarter, tiles):
                    if n is not None:
                        scores_ahead(n, quarter, tiles)

                def hidden(c):
                    def products(view, place, apart=False):
                        for m in range(M1):
                            pe.wait_ge(h_ready, b * (NCH * M1) + c * M1 + (m + 1))
                            if n is not None and isinstance(c, int) and c == 0 and hidden_bank(m) == 3:
                                pe.wait_ge(max_done, n * PAIRS + (2 + 2))
                            if apart:
                                carry(pe)
                            for k in range(2):
                                ins = nc.tensor.matmul(place(m), W1[:, k, m * P:(m + 1) * P], view(k),
                                                       start=(k == 0), stop=(k == 1))
                            ins.then_inc(fc1_done, 1)

                    def bank(m):
                        return PS[:, hidden_bank(m), :]

                    def columns(first):
                        return lambda k: XNT[:, k, bass.ds(first * HH, CH)]

                    with pe.If(direction >= 8):
                        products(lambda k: XNT[:, k, :].rearrange("p (w h) -> p h w", h=HH)[:, bass.ds(c * RW, RW), :], bank)
                    with pe.Else():
                        with pe.If(direction >= 2):
                            products(columns(c * RW), bank)
                        with pe.Else():
                            products(columns((NCH - 1 - c) * RW),
                                     lambda m: bank(m).rearrange("p (w h) -> p w h", h=HH)[:, ::-1, :], True)
                        pe.nop()
                    pe.nop()

                def project_out(c, s, between=()):
                    pe.wait_ge(gelu_done, b * NCH + c + 1)
                    pe.wait_ge(out_ready, b * NCH + c + 1)
                    for h in range(2):
                        for t in range(2):
                            for m in range(M1):
                                ins = nc.tensor.matmul(PS[:, 6 + h, t * C:(t + 1) * C],
                                                       T[:, s, m, (2 * h + t) * P:(2 * h + t + 1) * P], W2[:, m, :],
                                                       start=(m == 0), stop=(m == M1 - 1))
                        ins.then_inc(fc2_done, 1)
                        if h < len(between):
                            ahead(*between[h])

                hidden(0)
                ahead(0, (2, 3))
                hidden(1)
                ahead(0, (4, 5))
                if n is not None:
                    for copied in parts_copied[1:]:
                        pe.wait_ge(copied, n * 64 + 64)
                        carry(pe)
                with pe.Fori(0, NCH // 2 - 1) as i:
                    hidden(i * 2 + 2)
                    ahead(i + 1, (0,))
                    project_out(i * 2, 0, ((i + 1, (1,)), (i + 1, (2,))))
                    hidden(i * 2 + 3)
                    ahead(i + 1, (3,))
                    project_out(i * 2 + 1, 1, ((i + 1, (4,)), (i + 1, (5,))))
                project_out(NCH - 2, 0)
                if n is not None:
                    pe.wait_ge(h_ready, b * (NCH * M1) + (NCH * M1 + M1))
                    maximum_row(n, 0)
                project_out(NCH - 1, 1)

            turn(None, 0)
            v_by_key(0, NCH - 1)
            pe.wait_ge(xtc_a, NCH + 2)
            pe.wait_ge(xtc_v, NCH + 2)
            pe.wait_ge(first_loaded, 16)
            for unit in range(AHEAD):
                if unit % FIRST == 0:
                    pe.wait_ge(parts_copied[unit // FIRST], 64)
                scores_for_max(0, unit, unit % FIRST, unit // FIRST, 2 * (unit % 2), 1)
            maximum_row(0, 0)
            with pe.Fori(0, B - 1) as b:
                attention(b)
                turn(b, b + 1)
                feed_forward(b, b + 1)
            attention(B - 1)
            turn(B - 1, None)
            feed_forward(B - 1, None)


def kernel(**inputs):
    import numpy as np
    import concourse.bacc as bacc
    from concourse.bass_utils import run_bass_kernel_spmd

    a = {k: np.asarray(v) for k, v in inputs.items()}

    def halves(w):
        return np.ascontiguousarray(w.reshape(2, HC, -1).transpose(1, 0, 2))

    def tiles(w):
        return np.ascontiguousarray(w.reshape(M1, P, -1).transpose(1, 0, 2))

    def rows(w):
        return np.ascontiguousarray(np.broadcast_to(w.reshape(1, -1), (P, w.size)))

    f = np.float32
    wqkv = np.zeros((C, 3 * G), f)
    wqkv[:, 1:1 + D] = a["L0_conv_w_q"]
    wqkv[:, G + 1:G + 1 + D] = a["L0_conv_w_k"]
    wqkv[:, 2 * G:2 * G + D] = a["L0_conv_w_v"]
    wo = np.zeros((4, G, OW), f)
    wo[:, 0:D, 0:C] = a["L0_conv_w_o"]
    wo[:, D, C] = 1.0
    consts = np.zeros((4, P, P), f)
    p = np.arange(P)
    inner = p[(p % WW > 0) & (p % WW < WW - 1)]
    consts[0, p, p] = 1.0
    consts[1, inner + 1, inner] = 1.0
    consts[1, inner - 1, inner] = -1.0
    consts[2, p ^ WW, p] = 1.0
    consts[3, 0, 0:4] = (8.0, 4.0, 2.0, 1.0)
    arrays = dict(
        x=a["x"].reshape(B, L, C), wqkv=halves(wqkv), wo=wo.reshape(P, OW), gamma=rows(a["L0_conv_gamma"]),
        nwb=rows(a["L1_conv_norm_w"]), nwc=halves(a["L1_conv_norm_w"])[:, :, 0], nbc=halves(a["L1_conv_norm_b"])[:, :, 0],
        nb0=rows(a["L1_conv_norm_b"]),
        sw1=a["L1_conv_sel_w1"].T.reshape(1, 4, 16), sb1=a["L1_conv_sel_b1"].reshape(1, 16),
        sw2=a["L1_conv_sel_w2"].reshape(1, 4, 16), sb2=a["L1_conv_sel_b2"].reshape(1, 4),
        fc1=halves(a["L1_conv_fc1_w"].T), fc1b=tiles(a["L1_conv_fc1_b"])[:, :, 0], cw=tiles(a["L1_conv_conv_w"].reshape(DIN, 3)),
        cb=tiles(a["L1_conv_conv_b"])[:, :, 0], fc2=tiles(a["L1_conv_fc2_w"].T), fc2b=rows(a["L1_conv_fc2_b"]), consts=consts)
    nc = bacc.Bacc("TRN2", target_bir_lowering=False, num_devices=1)
    given, args = {}, {}
    for name, v in arrays.items():
        v = np.ascontiguousarray(v)
        given[f"in_{name}"] = v
        args[name] = nc.dram_tensor(f"in_{name}", v.shape, mybir.dt.from_np(v.dtype), kind="ExternalInput").ap()
    out = nc.dram_tensor("out_x", (B, L, C), F32, kind="ExternalOutput").ap()
    conv_seq_two_layers(nc, out=out, **args)
    r = run_bass_kernel_spmd(nc, [given], core_ids=[0])
    return r.results[0]["out_x"].reshape(B, HH, WW, C)
```
